# Optimizing a Trainium2 kernel written in Bass

```python
import numpy as np
import jax
import jax.numpy as jnp

def _softmax(x, axis=-1):
    return jax.nn.softmax(x, axis=axis)

def _gelu(x):
    return jax.nn.gelu(x, approximate=True)

def _silu(x):
    return jax.nn.silu(x)

def _sigmoid(x):
    return jax.nn.sigmoid(x)

def _layernorm(x, axis=-1, eps=1e-05):
    m = jnp.mean(x, axis=axis, keepdims=True)
    v = jnp.var(x, axis=axis, keepdims=True)
    return (x - m) / jnp.sqrt(v + eps)

def _scatter_add(tgt, idx, src, axis=0):
    return tgt.at[idx].add(src)

def _segment_sum(src, seg, n):
    return jax.ops.segment_sum(src, seg, n)
kernel_name = 'mk_seq_preln_d1_jaxref_r8_6fe0fc'

def setup_inputs(seed: int=0):
    np.random.seed(seed)
    _w = jnp.asarray

    def _L0_attn_setup():
        import jax, jax.numpy as jnp
        import numpy as np
        DIM = 128
        DIM_HEAD = 64
        N_HEADS = 16
        INNER = DIM_HEAD * N_HEADS
        LN_EPS = 1e-05

        def layer_norm(x, gamma, beta):
            mu = jnp.mean(x, axis=-1, keepdims=True)
            var = jnp.var(x, axis=-1, keepdims=True)
            return (x - mu) * jax.lax.rsqrt(var + LN_EPS) * gamma + beta

        def alibi_bias(seq, n_heads):
            n_sequence = jnp.arange(n_heads, 0, -1).astype(jnp.float32)
            head_scalars = 2.0 ** (-8.0 / n_sequence)
            idx = jnp.arange(seq)
            dist = -jnp.abs(idx[:, None] - idx[None, :]).astype(jnp.float32)
            return head_scalars[:, None, None] * dist
        key = jax.random.key(seed)
        ks = jax.random.split(key, 6)
        B, S = (2, 256)
        scale = 0.02
        return {'x': jax.random.normal(ks[0], (B, S, DIM), dtype=jnp.float32), 'ln_gamma': jnp.ones((DIM,), dtype=jnp.float32), 'ln_beta': jnp.zeros((DIM,), dtype=jnp.float32), 'Wq': jax.random.normal(ks[1], (DIM, INNER), dtype=jnp.float32) * scale, 'Wk': jax.random.normal(ks[2], (DIM, INNER), dtype=jnp.float32) * scale, 'Wv': jax.random.normal(ks[3], (DIM, INNER), dtype=jnp.float32) * scale, 'Wo': jax.random.normal(ks[4], (INNER, DIM), dtype=jnp.float32) * scale}
    _L0_attn_in = _L0_attn_setup()

    def _L0_ffn_setup():
        import jax, jax.numpy as jnp
        import numpy as np
        DIM = 128
        DEPTH = 2
        HEADS = 8
        DIM_HEAD = 64
        WINDOW = 64
        INNER = HEADS * DIM_HEAD
        HID = int(DIM * 4 * 2 / 3)
        B, N = (2, 1024)
        QK_SCALE = 8.0

        def shift_token(t):
            t1, t2 = jnp.split(t, 2, axis=-1)
            t2 = jnp.pad(t2, ((0, 0), (1, 0), (0, 0)))[:, :-1]
            return jnp.concatenate([t1, t2], axis=-1)

        def l2norm(t):
            return t / jnp.clip(jnp.linalg.norm(t, axis=-1, keepdims=True), 1e-12)

        def rotate_half(x):
            x1, x2 = jnp.split(x, 2, axis=-1)
            return jnp.concatenate([-x2, x1], axis=-1)

        def rotary_xpos(q, k):
            n = q.shape[-2]
            half_idx = jnp.arange(0, DIM_HEAD, 2, dtype=jnp.float32)
            inv_freq = 1.0 / 10000.0 ** (half_idx / DIM_HEAD)
            t = jnp.arange(n, dtype=jnp.float32)
            freqs = t[:, None] * inv_freq[None, :]
            freqs = jnp.concatenate([freqs, freqs], axis=-1)
            base = (half_idx + 0.4 * DIM_HEAD) / (1.4 * DIM_HEAD)
            power = (t - n // 2) / float(WINDOW // 2)
            scale = base[None, :] ** power[:, None]
            scale = jnp.concatenate([scale, scale], axis=-1)
            cos, sin = (jnp.cos(freqs), jnp.sin(freqs))
            q = q * cos * scale + rotate_half(q) * sin * scale
            k = k * cos / scale + rotate_half(k) * sin / scale
            return (q, k)

        def local_attention(q, k, v):
            b, h, n, d = q.shape
            w = n // WINDOW
            bq = q.reshape(b, h, w, WINDOW, d) * QK_SCALE
            bk = k.reshape(b, h, w, WINDOW, d)
            bv = v.reshape(b, h, w, WINDOW, d)

            def look_around(t):
                p = jnp.pad(t, ((0, 0), (0, 0), (1, 0), (0, 0), (0, 0)))
                return jnp.concatenate([p[:, :, :w], p[:, :, 1:]], axis=3)
            bk, bv = (look_around(bk), look_around(bv))
            bt = jnp.arange(n).reshape(w, WINDOW)
            btp = jnp.pad(bt, ((1, 0), (0, 0)), constant_values=-1)
            btk = jnp.concatenate([btp[:w], btp[1:]], axis=1)
            sim = jnp.einsum('bhwid,bhwjd->bhwij', bq, bk)
            i = bt[:, :, None]
            j = btk[:, None, :]
            mask = (i < j) | (i > j + WINDOW) | (j == -1)
            sim = jnp.where(mask, -jnp.finfo(sim.dtype).max, sim)
            attn = jax.nn.softmax(sim, axis=-1)
            out = jnp.einsum('bhwij,bhwjd->bhwid', attn, bv)
            return out.reshape(b, h, n, d)

        def _layer(x, wqkv, qs, ksc, wo, lg, lb, w1, b1, w2, b2):
            b, n, _ = x.shape
            h = shift_token(x)
            qkv = h @ wqkv
            q, k, v = jnp.split(qkv, 3, axis=-1)
            to_heads = lambda t: t.reshape(b, n, HEADS, DIM_HEAD).transpose(0, 2, 1, 3)
            q, k, v = (to_heads(q), to_heads(k), to_heads(v))
            q = l2norm(q) * qs
            k = l2norm(k) * ksc
            q, k = rotary_xpos(q, k)
            o = local_attention(q, k, v)
            o = o.transpose(0, 2, 1, 3).reshape(b, n, INNER)
            x = x + o @ wo
            h = shift_token(x)
            mu = h.mean(-1, keepdims=True)
            var = h.var(-1, keepdims=True)
            h = (h - mu) / jnp.sqrt(var + 1e-05) * lg + lb
            h = h @ w1 + b1
            a, g = jnp.split(h, 2, axis=-1)
            h = a * jax.nn.gelu(g, approximate=False)
            x = x + h @ w2 + b2
            return x
        key = jax.random.key(seed)
        ks = jax.random.split(key, 6)
        return {'x': jax.random.normal(ks[0], (B, N, DIM), jnp.float32), 'wqkv': jax.random.normal(ks[1], (DEPTH, DIM, 3 * INNER), jnp.float32) * 0.02, 'q_scale': jnp.ones((DEPTH, DIM_HEAD), jnp.float32), 'k_scale': jnp.ones((DEPTH, DIM_HEAD), jnp.float32), 'wo': jax.random.normal(ks[2], (DEPTH, INNER, DIM), jnp.float32) * 0.02, 'ln_g': jnp.ones((DEPTH, DIM), jnp.float32), 'ln_b': jnp.zeros((DEPTH, DIM), jnp.float32), 'w1': jax.random.normal(ks[3], (DEPTH, DIM, 2 * HID), jnp.float32) * 0.02, 'b1': jnp.zeros((DEPTH, 2 * HID), jnp.float32), 'w2': jax.random.normal(ks[4], (DEPTH, HID, DIM), jnp.float32) * 0.02, 'b2': jnp.zeros((DEPTH, DIM), jnp.float32)}
    _L0_ffn_in = _L0_ffn_setup()
    _d = {'L0_attn_x': _L0_attn_in['x'], 'L0_attn_ln_gamma': _L0_attn_in['ln_gamma'], 'L0_attn_ln_beta': _L0_attn_in['ln_beta'], 'L0_attn_Wq': _L0_attn_in['Wq'], 'L0_attn_Wk': _L0_attn_in['Wk'], 'L0_attn_Wv': _L0_attn_in['Wv'], 'L0_attn_Wo': _L0_attn_in['Wo'], 'L0_ffn_wqkv': _L0_ffn_in['wqkv'], 'L0_ffn_q_scale': _L0_ffn_in['q_scale'], 'L0_ffn_k_scale': _L0_ffn_in['k_scale'], 'L0_ffn_wo': _L0_ffn_in['wo'], 'L0_ffn_ln_g': _L0_ffn_in['ln_g'], 'L0_ffn_ln_b': _L0_ffn_in['ln_b'], 'L0_ffn_w1': _L0_ffn_in['w1'], 'L0_ffn_b1': _L0_ffn_in['b1'], 'L0_ffn_w2': _L0_ffn_in['w2'], 'L0_ffn_b2': _L0_ffn_in['b2']}
    _x0 = _d['L0_attn_x']
    _d['L0_attn_x'] = jax.random.normal(jax.random.fold_in(jax.random.key(seed), 1), (16, 512, 128), dtype=_x0.dtype)
    del _x0
    return _d

def reference(L0_attn_x, L0_attn_ln_gamma, L0_attn_ln_beta, L0_attn_Wq, L0_attn_Wk, L0_attn_Wv, L0_attn_Wo, L0_ffn_wqkv, L0_ffn_q_scale, L0_ffn_k_scale, L0_ffn_wo, L0_ffn_ln_g, L0_ffn_ln_b, L0_ffn_w1, L0_ffn_b1, L0_ffn_w2, L0_ffn_b2):

    def _L0_attn_ref(x, ln_gamma, ln_beta, Wq, Wk, Wv, Wo):
        import jax, jax.numpy as jnp
        import numpy as np
        DIM = 128
        DIM_HEAD = 64
        N_HEADS = 16
        INNER = DIM_HEAD * N_HEADS
        LN_EPS = 1e-05

        def layer_norm(x, gamma, beta):
            mu = jnp.mean(x, axis=-1, keepdims=True)
            var = jnp.var(x, axis=-1, keepdims=True)
            return (x - mu) * jax.lax.rsqrt(var + LN_EPS) * gamma + beta

        def alibi_bias(seq, n_heads):
            n_sequence = jnp.arange(n_heads, 0, -1).astype(jnp.float32)
            head_scalars = 2.0 ** (-8.0 / n_sequence)
            idx = jnp.arange(seq)
            dist = -jnp.abs(idx[:, None] - idx[None, :]).astype(jnp.float32)
            return head_scalars[:, None, None] * dist
        B, S, _ = x.shape
        xn = layer_norm(x, ln_gamma, ln_beta)

        def heads(t):
            return t.reshape(B, S, N_HEADS, DIM_HEAD).transpose(0, 2, 1, 3)
        q = heads(xn @ Wq)
        k = heads(xn @ Wk)
        v = heads(xn @ Wv)
        att = jnp.einsum('bhid,bhjd->bhij', q, k) / DIM_HEAD ** 0.5
        att = att + alibi_bias(S, N_HEADS)[None]
        p = jax.nn.softmax(att, axis=-1)
        out = jnp.einsum('bhij,bhjd->bhid', p, v)
        out = out.transpose(0, 2, 1, 3).reshape(B, S, INNER)
        return out @ Wo

    def _L0_ffn_ref(x, wqkv, q_scale, k_scale, wo, ln_g, ln_b, w1, b1, w2, b2):
        import jax, jax.numpy as jnp
        import numpy as np
        DIM = 128
        DEPTH = 2
        HEADS = 8
        DIM_HEAD = 64
        WINDOW = 64
        INNER = HEADS * DIM_HEAD
        HID = int(DIM * 4 * 2 / 3)
        B, N = (2, 1024)
        QK_SCALE = 8.0

        def shift_token(t):
            t1, t2 = jnp.split(t, 2, axis=-1)
            t2 = jnp.pad(t2, ((0, 0), (1, 0), (0, 0)))[:, :-1]
            return jnp.concatenate([t1, t2], axis=-1)

        def l2norm(t):
            return t / jnp.clip(jnp.linalg.norm(t, axis=-1, keepdims=True), 1e-12)

        def rotate_half(x):
            x1, x2 = jnp.split(x, 2, axis=-1)
            return jnp.concatenate([-x2, x1], axis=-1)

        def rotary_xpos(q, k):
            n = q.shape[-2]
            half_idx = jnp.arange(0, DIM_HEAD, 2, dtype=jnp.float32)
            inv_freq = 1.0 / 10000.0 ** (half_idx / DIM_HEAD)
            t = jnp.arange(n, dtype=jnp.float32)
            freqs = t[:, None] * inv_freq[None, :]
            freqs = jnp.concatenate([freqs, freqs], axis=-1)
            base = (half_idx + 0.4 * DIM_HEAD) / (1.4 * DIM_HEAD)
            power = (t - n // 2) / float(WINDOW // 2)
            scale = base[None, :] ** power[:, None]
            scale = jnp.concatenate([scale, scale], axis=-1)
            cos, sin = (jnp.cos(freqs), jnp.sin(freqs))
            q = q * cos * scale + rotate_half(q) * sin * scale
            k = k * cos / scale + rotate_half(k) * sin / scale
            return (q, k)

        def local_attention(q, k, v):
            b, h, n, d = q.shape
            w = n // WINDOW
            bq = q.reshape(b, h, w, WINDOW, d) * QK_SCALE
            bk = k.reshape(b, h, w, WINDOW, d)
            bv = v.reshape(b, h, w, WINDOW, d)

            def look_around(t):
                p = jnp.pad(t, ((0, 0), (0, 0), (1, 0), (0, 0), (0, 0)))
                return jnp.concatenate([p[:, :, :w], p[:, :, 1:]], axis=3)
            bk, bv = (look_around(bk), look_around(bv))
            bt = jnp.arange(n).reshape(w, WINDOW)
            btp = jnp.pad(bt, ((1, 0), (0, 0)), constant_values=-1)
            btk = jnp.concatenate([btp[:w], btp[1:]], axis=1)
            sim = jnp.einsum('bhwid,bhwjd->bhwij', bq, bk)
            i = bt[:, :, None]
            j = btk[:, None, :]
            mask = (i < j) | (i > j + WINDOW) | (j == -1)
            sim = jnp.where(mask, -jnp.finfo(sim.dtype).max, sim)
            attn = jax.nn.softmax(sim, axis=-1)
            out = jnp.einsum('bhwij,bhwjd->bhwid', attn, bv)
            return out.reshape(b, h, n, d)

        def _layer(x, wqkv, qs, ksc, wo, lg, lb, w1, b1, w2, b2):
            b, n, _ = x.shape
            h = shift_token(x)
            qkv = h @ wqkv
            q, k, v = jnp.split(qkv, 3, axis=-1)
            to_heads = lambda t: t.reshape(b, n, HEADS, DIM_HEAD).transpose(0, 2, 1, 3)
            q, k, v = (to_heads(q), to_heads(k), to_heads(v))
            q = l2norm(q) * qs
            k = l2norm(k) * ksc
            q, k = rotary_xpos(q, k)
            o = local_attention(q, k, v)
            o = o.transpose(0, 2, 1, 3).reshape(b, n, INNER)
            x = x + o @ wo
            h = shift_token(x)
            mu = h.mean(-1, keepdims=True)
            var = h.var(-1, keepdims=True)
            h = (h - mu) / jnp.sqrt(var + 1e-05) * lg + lb
            h = h @ w1 + b1
            a, g = jnp.split(h, 2, axis=-1)
            h = a * jax.nn.gelu(g, approximate=False)
            x = x + h @ w2 + b2
            return x
        for l in range(DEPTH):
            x = _layer(x, wqkv[l], q_scale[l], k_scale[l], wo[l], ln_g[l], ln_b[l], w1[l], b1[l], w2[l], b2[l])
        return x
    x = L0_attn_x
    x = x + _L0_attn_ref(_layernorm(x, axis=-1), L0_attn_ln_gamma, L0_attn_ln_beta, L0_attn_Wq, L0_attn_Wk, L0_attn_Wv, L0_attn_Wo)
    x = x + _L0_ffn_ref(_layernorm(x, axis=-1), L0_ffn_wqkv, L0_ffn_q_scale, L0_ffn_k_scale, L0_ffn_wo, L0_ffn_ln_g, L0_ffn_ln_b, L0_ffn_w1, L0_ffn_b1, L0_ffn_w2, L0_ffn_b2)
    return x

_drawn_inputs = setup_inputs


def setup_inputs(seed=0):
    import zlib

    import numpy as np

    out = dict(_drawn_inputs(seed))
    spreads = {'L0_attn_ln_gamma': (1.0, 0.6),
     'L0_attn_ln_beta': (0.0, 0.5),
     'L0_ffn_q_scale': (1.0, 0.6),
     'L0_ffn_k_scale': (1.0, 0.6),
     'L0_ffn_ln_g': (1.0, 0.6),
     'L0_ffn_ln_b': (0.0, 0.8),
     'L0_ffn_b1': (0.0, 0.8),
     'L0_ffn_b2': (0.0, 0.436)}
    factors = {'L0_attn_Wq': 8.0,
     'L0_attn_Wk': 8.0,
     'L0_ffn_wqkv': 3.72,
     'L0_ffn_wo': 3.724,
     'L0_ffn_w1': 6.168,
     'L0_ffn_w2': 6.085}
    for name, (base, spread) in spreads.items():
        noise = np.random.default_rng([zlib.crc32(name.encode()), seed]).standard_normal(out[name].shape)
        drawn = base * np.exp(spread * noise) if base else spread * noise
        out[name] = jnp.asarray(drawn.astype(out[name].dtype))
    for name, factor in factors.items():
        out[name] = (out[name] * factor).astype(out[name].dtype)
    return out
```

```python
from contextlib import ExitStack

import concourse.bass as bass
from concourse import mybir

ALU = mybir.AluOpType
ACT = mybir.ActivationFunctionType
F32 = mybir.dt.float32
AX = mybir.AxisListType

P = 128
NB, S, D = 16, 512, 128
NT = S // P
TILES = NB * NT
DH = 64
NH = 16
NPAIR = NH // 2
FH = 8
FPAIR = FH // 2
W = 64
NW = S // W
DEPTH = 2
HID = 341
DW = S + (NT - 1) * P
EPS = 1e-5
SCALE = float(DH) ** -0.5
CH = [(0, 128), (128, 128), (256, HID - 256)]
LOW = -3.0e38


def layer_stats(nc, ctx, name, src, mean, rstd, work, twice):
    stats_done = ctx.enter_context(nc.semaphore(name + "_stats_done"))
    var_done = ctx.enter_context(nc.semaphore(name + "_var_done"))
    root_done = ctx.enter_context(nc.semaphore(name + "_root_done"))
    fac_done = ctx.enter_context(nc.semaphore(name + "_fac_done"))
    stats, mv, root, fac = work
    with nc.Block() as block:

        @block.vector
        def _(dve):
            for t in range(TILES):
                ins = nc.vector.bn_stats(stats[:, t, :], src[:, t, :])
            ins.then_inc(stats_done, 1)
            dve.wait_ge(stats_done, 1)
            for t in range(TILES):
                ins = nc.vector.bn_aggr(mv[:, t, :], stats[:, t, :])
            ins.then_inc(stats_done, 1)
            dve.wait_ge(stats_done, 2)
            nc.vector.tensor_copy(mean[:], mv[:, :, 0])
            nc.vector.tensor_scalar(fac[:], mv[:, :, 1], EPS, None, ALU.add).then_inc(var_done, 1)
            dve.wait_ge(root_done, 1)
            nc.vector.reciprocal(rstd[:], root[:]).then_inc(fac_done, 1)
            dve.wait_ge(fac_done, 1)
            if twice:
                nc.vector.tensor_tensor(fac[:], rstd[:], rstd[:], ALU.mult).then_inc(fac_done, 1)
                dve.wait_ge(fac_done, 2)
                nc.vector.tensor_tensor(fac[:], fac[:], mv[:, :, 1], ALU.mult).then_inc(fac_done, 1)
                dve.wait_ge(fac_done, 3)
                nc.vector.tensor_scalar(fac[:], fac[:], EPS, None, ALU.add).then_inc(var_done, 1)
                dve.wait_ge(root_done, 2)
                nc.vector.reciprocal(fac[:], root[:]).then_inc(fac_done, 1)
                dve.wait_ge(fac_done, 4)
                nc.vector.tensor_tensor(rstd[:], rstd[:], fac[:], ALU.mult).then_inc(fac_done, 1)

        @block.scalar
        def _(act):
            act.wait_ge(var_done, 1)
            nc.scalar.activation(root[:], fac[:], ACT.Sqrt).then_inc(root_done, 1)
            if twice:
                act.wait_ge(var_done, 2)
                nc.scalar.activation(root[:], fac[:], ACT.Sqrt).then_inc(root_done, 1)


def global_attention(nc, ctx, X, mean, rstd, ident, dist, gb, wqkv, wo):
    def sb(name, shape):
        return ctx.enter_context(nc.sbuf_tensor(name, shape, F32))

    def ps(name, shape):
        return ctx.enter_context(nc.psum_tensor(name, shape, F32))

    sems = []

    def sem(name):
        sems.append(ctx.enter_context(nc.semaphore(name)))
        return sems[-1]

    xs = sb("xs", [P, NT, D])
    xnT = sb("xnT", [P, S])
    V = sb("V", [P, NT, NH * DH])
    qz = sb("qz", [P, 2, 2, S])
    kT = sb("kT", [P, 2, S])
    tab = sb("tab", [P, 4, DW])
    biased = sb("biased", [P, 2, S])
    negmax = sb("negmax", [P, NPAIR * 8])
    prob = sb("prob", [P, 2, 8, S])
    sums = sb("sums", [P, NPAIR, 2, NT])
    rinv = sb("rinv", [P, NPAIR, 2, NT])
    PT = sb("PT", [P, 2, 4, S])
    Rs = sb("Rs", [P, 2, S])
    oT = sb("oT", [P, NPAIR, S])

    sc_ps = ps("sc_ps", [P, 3, S])
    pt_ps = ps("pt_ps", [P, 2, S])
    o_ps = ps("o_ps", [P, S])
    m_ps = ps("m_ps", [P, 2, S])

    xs_ready = sem("xs_ready")
    xT_ready = sem("xT_ready")
    xn_ready = sem("xn_ready")
    v_done = sem("v_done")
    v_copied = sem("v_copied")
    q_done = sem("q_done")
    k_done = sem("k_done")
    q_copied = sem("q_copied")
    k_copied = sem("k_copied")
    tab_ready = sem("tab_ready")
    score_done = sem("score_done")
    biased_done = sem("biased_done")
    exp_done = sem("exp_done")
    turned = [sem("turned_a"), sem("turned_b")]
    pt_copied = [sem("pt_copied_act"), sem("pt_copied_dve")]
    pv_done = sem("pv_done")
    rinv_ready = sem("rinv_ready")
    r_done = sem("r_done")
    r_copied = sem("r_copied")
    out_scaled = sem("out_scaled")
    wo_done = sem("wo_done")
    x_added = sem("x_added")
    zeroed = sem("zeroed")

    NS = NPAIR * 8
    NK = NPAIR * NT

    with nc.Block() as block:
        @block.vector
        def _(dve):
            nc.vector.memset(qz[:], 0.0).then_inc(zeroed, 1)
            dve.wait_ge(zeroed, 1)

    with nc.Fori(0, NB) as b:
        with nc.Block() as block:

            @block.gpsimd
            def _(pool):
                for h in range(NH):
                    if h >= 4:
                        pool.wait_ge(biased_done, 4 * (h - 3))
                    slope = 2.0 ** (-8.0 / (NH - h))
                    nc.gpsimd.tensor_scalar(tab[:, h % 4, :], dist[:], -slope / SCALE, None,
                                            ALU.mult).then_inc(tab_ready, 1)

            @block.tensor
            def _(pe):
                pe.wait_ge(xs_ready, 1)
                for j in range(NT):
                    ins = nc.tensor.transpose(m_ps[:, 0, j * P:(j + 1) * P], xs[:, j, :], ident[:])
                ins.then_inc(xT_ready, 1)
                pe.wait_ge(xn_ready, 1)
                for n in range(2 * NT):
                    j, half = n // 2, n % 2
                    if n >= 1:
                        pe.wait_ge(v_copied, n - 1)
                    nc.tensor.matmul(m_ps[:, (n + 1) % 2, :], xnT[:, j * P:(j + 1) * P],
                                     wqkv[:, 2 * NH * DH + half * S:2 * NH * DH + (half + 1) * S],
                                     start=True, stop=True).then_inc(v_done, 1)

                def project(p):
                    if p == 0:
                        pe.wait_ge(v_copied, 2 * NT)
                    else:
                        pe.wait_ge(k_copied, p)
                        pe.wait_ge(q_copied, p)
                    if p >= 3:
                        pe.wait_ge(r_copied, p - 2)
                    nc.tensor.matmul(m_ps[:, 0, :], wqkv[:, p * P:(p + 1) * P], xnT[:],
                                     start=True, stop=True).then_inc(q_done, 1)
                    nc.tensor.matmul(m_ps[:, 1, :], wqkv[:, NH * DH + p * P:NH * DH + (p + 1) * P], xnT[:],
                                     start=True, stop=True).then_inc(k_done, 1)

                def scores(p, i):
                    h, q = i // NT, i % NT
                    n = p * 8 + i
                    if i == 0:
                        pe.wait_ge(q_copied, p + 1)
                        pe.wait_ge(k_copied, p + 1)
                    if n > 2:
                        pe.wait_ge(biased_done, n - 2)
                    nc.tensor.matmul(sc_ps[:, n % 3, :], qz[:, p % 2, h, q * P:(q + 1) * P], kT[:, p % 2, :],
                                     start=True, stop=True).then_inc(score_done, 1)

                def turn(p, i):
                    k, h = i // 2, i % 2
                    if k == 0:
                        pe.wait_ge(exp_done, p * 8 + 4 * h + 4)
                    pe.wait_ge(pt_copied[h], p * NT + k)
                    for q in range(NT):
                        ins = nc.tensor.transpose(pt_ps[:, h, q * P:(q + 1) * P],
                                                  prob[:, p % 2, 4 * h + q, k * P:(k + 1) * P], ident[:])
                    ins.then_inc(turned[h], 1)

                def mix(p, k):
                    n = p * NT + k
                    pe.wait_ge(pt_copied[0], n + 1)
                    pe.wait_ge(pt_copied[1], n + 1)
                    if k == 0:
                        pe.wait_ge(out_scaled, p)
                    for h in range(2):
                        c = (2 * p + h) * DH
                        ins = nc.tensor.matmul(o_ps[h * DH:(h + 1) * DH, :], V[:, k, c:c + DH], PT[:, h, n % 4, :],
                                               start=(k == 0), stop=(k == NT - 1))
                    ins.then_inc(pv_done, 1)

                project(0)
                for p in range(-1, NPAIR):
                    for i in range(8):
                        if p + 1 < NPAIR:
                            scores(p + 1, i)
                        if p >= 0:
                            turn(p, i)
                            if i % 2 == 1 and i > 1:
                                mix(p, i // 2 - 1)
                        if i == 4 and p + 2 < NPAIR:
                            project(p + 2)
                    if p >= 0:
                        pe.wait_ge(rinv_ready, p + 1)
                        last = min(p + 3, NPAIR)
                        pe.wait_ge(k_copied, last)
                        pe.wait_ge(q_copied, last)
                        pe.wait_ge(r_copied, p)
                        for q in range(NT):
                            for h in range(2):
                                ins = nc.tensor.matmul(m_ps[h * DH:(h + 1) * DH, 0, q * P:(q + 1) * P],
                                                       rinv[:, p, h, q:q + 1].broadcast_to([P, DH]), ident[:],
                                                       start=True, stop=True)
                        ins.then_inc(r_done, 1)
                        mix(p, NT - 1)
                pe.wait_ge(out_scaled, NPAIR)
                for q in range(NT):
                    for p in range(NPAIR):
                        ins = nc.tensor.matmul(m_ps[:, 1, q * P:(q + 1) * P], oT[:, p, q * P:(q + 1) * P],
                                               wo[:, p, :], start=(p == 0), stop=(p == NPAIR - 1))
                ins.then_inc(wo_done, 1)

            @block.scalar
            def _(act):
                act.wait_ge(xT_ready, 1)
                nc.scalar.activation(xnT[:], m_ps[:, 0, :], ACT.Identity, bias=gb[:, 1:2],
                                     scale=gb[:, 0:1]).then_inc(xn_ready, 1)
                for n in range(2 * NT):
                    j, half = n // 2, n % 2
                    act.wait_ge(v_done, n + 1)
                    nc.scalar.activation(V[:, j, half * S:(half + 1) * S], m_ps[:, (n + 1) % 2, :],
                                         ACT.Copy).then_inc(v_copied, 1)

                def key_copy(p):
                    act.wait_ge(k_done, p + 1)
                    if p >= 2:
                        act.wait_ge(score_done, 8 * (p - 1))
                    nc.scalar.activation(kT[:, p % 2, :], m_ps[:, 1, :], ACT.Copy).then_inc(k_copied, 1)

                key_copy(0)
                for p in range(-1, NPAIR):
                    for i in range(8):
                        if p + 1 < NPAIR:
                            n = (p + 1) * 8 + i
                            act.wait_ge(biased_done, n + 1)
                            if i == 0 and p >= 1:
                                act.wait_ge(turned[0], p * NT)
                                act.wait_ge(turned[1], p * NT)
                            nc.scalar.activation(prob[:, (p + 1) % 2, i, :], biased[:, n % 2, :], ACT.Exp,
                                                 bias=negmax[:, n:n + 1], scale=-1.0,
                                                 accum_out=sums[:, p + 1, i // NT, i % NT:i % NT + 1])\
                                .then_inc(exp_done, 1)
                        if p >= 0 and i % 2 == 0:
                            n = p * NT + i // 2
                            act.wait_ge(turned[0], n + 1)
                            if n > 3:
                                act.wait_ge(pv_done, n - 3)
                            nc.scalar.activation(PT[:, 0, n % 4, :], pt_ps[:, 0, :], ACT.Copy)\
                                .then_inc(pt_copied[0], 1)
                        if i == 4 and p + 2 < NPAIR:
                            key_copy(p + 2)
                    if p >= 0:
                        act.wait_ge(r_done, p + 1)
                        if p > 1:
                            act.wait_ge(out_scaled, p - 1)
                        nc.scalar.activation(Rs[:, p % 2, :], m_ps[:, 0, :], ACT.Copy).then_inc(r_copied, 1)

            @block.vector
            def _(dve):
                for j in range(NT):
                    t = b * NT + j
                    ins = nc.vector.tensor_scalar(xs[:, j, :], X[:, bass.ds(t, 1), :], mean[:, bass.ds(t, 1)],
                                                  rstd[:, bass.ds(t, 1)], ALU.subtract, ALU.mult)
                ins.then_inc(xs_ready, 1)

                def query_copy(p):
                    dve.wait_ge(q_done, p + 1)
                    if p >= 2:
                        dve.wait_ge(score_done, 8 * (p - 1))
                    for h in range(2):
                        r = slice(h * DH, (h + 1) * DH)
                        ins = nc.vector.tensor_copy(qz[r, p % 2, h, :], m_ps[r, 0, :])
                    ins.then_inc(q_copied, 1)

                query_copy(0)
                for p in range(-1, NPAIR):
                    if p >= 0:
                        dve.wait_ge(exp_done, 8 * (p + 1))
                        nc.vector.reciprocal(rinv[:, p, :, :], sums[:, p, :, :]).then_inc(rinv_ready, 1)
                    for i in range(8):
                        if p + 1 < NPAIR:
                            n = (p + 1) * 8 + i
                            h, q = i // NT, i % NT
                            head = 2 * (p + 1) + h
                            dve.wait_ge(score_done, n + 1)
                            if q == 0:
                                dve.wait_ge(tab_ready, head + 1)
                            if n > 1:
                                dve.wait_ge(exp_done, n - 1)
                            c = (NT - 1 - q) * P
                            nc.vector.tensor_tensor_reduce(
                                out=biased[:, n % 2, :], in0=sc_ps[:, n % 3, :], in1=tab[:, head % 4, c:c + S],
                                scale=-SCALE, scalar=-LOW, op0=ALU.add, op1=ALU.min,
                                accum_out=negmax[:, n:n + 1]).then_inc(biased_done, 1)
                        if p >= 0 and i % 2 == 1:
                            n = p * NT + i // 2
                            dve.wait_ge(turned[1], n + 1)
                            if n > 3:
                                dve.wait_ge(pv_done, n - 3)
                            nc.vector.tensor_copy(PT[:, 1, n % 4, :], pt_ps[:, 1, :]).then_inc(pt_copied[1], 1)
                        if i == 4 and p + 2 < NPAIR:
                            query_copy(p + 2)
                    if p >= 0:
                        dve.wait_ge(r_copied, p + 1)
                        dve.wait_ge(pv_done, (p + 1) * NT)
                        nc.vector.tensor_tensor(oT[:, p, :], o_ps[:], Rs[:, p % 2, :], ALU.mult)\
                            .then_inc(out_scaled, 1)
                dve.wait_ge(wo_done, 1)
                mine = X[:, bass.ds(b * NT, NT), :]
                nc.vector.tensor_tensor(mine, m_ps[:, 1, :].rearrange("p (j d) -> p j d", j=NT), mine,
                                        ALU.add).then_inc(x_added, 1)
        for s in sems:
            nc.gpsimd.sem_clear(s)
        nc.all_engine_barrier()


def local_attention(nc, ctx, tag, H, ident, mask, ropeC, ropeS, wqkv, wo):
    def sb(name, shape):
        return ctx.enter_context(nc.sbuf_tensor(tag + name, shape, F32))

    def ps(name, shape):
        return ctx.enter_context(nc.psum_tensor(tag + name, shape, F32))

    sems = []

    def sem(name):
        sems.append(ctx.enter_context(nc.semaphore(tag + name)))
        return sems[-1]

    QK = 2 * FH * DH
    hs = sb("hs", [P, NT, D])
    hT = sb("hT", [P, W + S])
    V = sb("V", [P, NW, FH * DH])
    raw = sb("raw", [P, NT, QK])
    sq = sb("sq", [P, QK])
    t1 = sb("t1", [P, 2, QK])
    t2 = sb("t2", [P, QK])
    ss = sb("ss", [P, NT, 2 * FH])
    rn = sb("rn", [P, NT, 2 * FH])
    qT = sb("qT", [P, FPAIR, S])
    kT = sb("kT", [P, FPAIR, W + S])
    biased = sb("biased", [P, 2, S])
    negmax = sb("negmax", [P, FH, NT])
    prob = sb("prob", [P, 2, S])
    sums = sb("sums", [P, FH, NT])
    rinv = sb("rinv", [P, FH, NT])
    PT = sb("PT", [P, 2, S])
    Rs = sb("Rs", [P, S])
    oT = sb("oT", [P, FPAIR, S])

    qk_ps = ps("qk_ps", [P, 2, S])
    m_ps = ps("m_ps", [P, 2, S])
    s_ps = ps("s_ps", [P, 2, S])
    pt_ps = ps("pt_ps", [P, S])
    o_ps = ps("o_ps", [P, S])

    hs_ready = sem("hs_ready")
    h_turned = sem("h_turned")
    hT_ready = sem("hT_ready")
    v_done = sem("v_done")
    v_copied = sem("v_copied")
    qk_done = sem("qk_done")
    raw_ready = sem("raw_ready")
    sq_ready = sem("sq_ready")
    ss_ready = sem("ss_ready")
    root_ready = sem("root_ready")
    rn_ready = sem("rn_ready")
    t1_ready = sem("t1_ready")
    t2_ready = sem("t2_ready")
    rot_done = sem("rot_done")
    qk_scaled = sem("qk_scaled")
    qk_turned = sem("qk_turned")
    qkT_ready = sem("qkT_ready")
    score_done = sem("score_done")
    biased_done = sem("biased_done")
    exp_done = sem("exp_done")
    p_turned = sem("p_turned")
    pt_copied = sem("pt_copied")
    pv_done = sem("pv_done")
    rinv_ready = sem("rinv_ready")
    r_done = sem("r_done")
    r_copied = sem("r_copied")
    out_scaled = sem("out_scaled")
    wo_done = sem("wo_done")
    h_added = sem("h_added")
    zeroed = sem("zeroed")

    with nc.Block() as block:
        @block.vector
        def _(dve):
            nc.vector.memset(hT[:], 0.0)
            nc.vector.memset(kT[:, :, 0:W], 0.0).then_inc(zeroed, 1)
            dve.wait_ge(zeroed, 1)

    with nc.Fori(0, NB) as b:
        with nc.Block() as block:

            @block.gpsimd
            def _(pool):
                nc.gpsimd.tensor_copy(hs[:], H[:, bass.ds(b * NT, NT), :]).then_inc(hs_ready, 1)
                for j in range(NT):
                    pool.wait_ge(raw_ready, j + 1)
                    if j >= 2:
                        pool.wait_ge(rot_done, j - 1)
                    for s in range(2):
                        c = slice(s * FH * DH, (s + 1) * FH * DH)
                        ins = nc.gpsimd.tensor_tensor(
                            t1[:, j % 2, c].rearrange("p (h d) -> p h d", d=DH),
                            raw[:, j, c].rearrange("p (h d) -> p h d", d=DH),
                            ropeC[:, j, s:s + 1, :].broadcast_to([P, FH, DH]), ALU.mult)
                    ins.then_inc(t1_ready, 1)

            @block.tensor
            def _(pe):
                pe.wait_ge(hs_ready, 1)
                for j in range(NT):
                    ins = nc.tensor.transpose(m_ps[:, 0, j * P:(j + 1) * P], hs[:, j, :], ident[:])
                ins.then_inc(h_turned, 1)
                pe.wait_ge(hT_ready, 2)
                for j in range(NT):
                    pe.wait_ge(raw_ready, j)
                    pe.wait_ge(sq_ready, j)
                    for s in range(2):
                        ins = nc.tensor.matmul(qk_ps[:, s, :], hT[:, W + j * P:W + (j + 1) * P],
                                               wqkv[:, s * S:(s + 1) * S], start=True, stop=True)
                    ins.then_inc(qk_done, 1)
                for w in range(NW):
                    if w > 1:
                        pe.wait_ge(v_copied, w - 1)
                    nc.tensor.matmul(m_ps[:, w % 2, :], hT[:, w * W:w * W + P], wqkv[:, 2 * S:3 * S],
                                     start=True, stop=True).then_inc(v_done, 1)
                for j in range(NT):
                    pe.wait_ge(qk_scaled, j + 1)
                    for s in range(2):
                        n = 2 * j + s
                        if n == 0:
                            pe.wait_ge(v_copied, NW)
                        if n > 1:
                            pe.wait_ge(qkT_ready, n - 1)
                        for c in range(FPAIR):
                            ins = nc.tensor.transpose(m_ps[:, s, c * P:(c + 1) * P],
                                                      raw[:, j, s * S + c * P:s * S + (c + 1) * P], ident[:])
                        ins.then_inc(qk_turned, 1)
                pe.wait_ge(qkT_ready, 2 * NT)

                def scores(h):
                    r = slice((h % 2) * DH, (h % 2 + 1) * DH)
                    if h > 1:
                        pe.wait_ge(biased_done, h - 1)
                    for w in range(NW):
                        o = (w % 2) * W
                        ins = nc.tensor.matmul(s_ps[o:o + W, h % 2, (w // 2) * P:(w // 2 + 1) * P],
                                               qT[r, h // 2, w * W:(w + 1) * W],
                                               kT[r, h // 2, w * W:w * W + P], start=True, stop=True)
                    ins.then_inc(score_done, 1)

                scores(0)
                for h in range(FH):
                    if h + 1 < FH:
                        scores(h + 1)
                    pe.wait_ge(exp_done, h + 1)
                    pe.wait_ge(pt_copied, h)
                    for u in range(NT):
                        ins = nc.tensor.transpose(pt_ps[:, u * P:(u + 1) * P],
                                                  prob[:, h % 2, u * P:(u + 1) * P], ident[:])
                    ins.then_inc(p_turned, 1)
                    pe.wait_ge(pt_copied, h + 1)
                    if h % 2 == 0:
                        pe.wait_ge(out_scaled, h // 2)
                    for w in range(NW):
                        ins = nc.tensor.matmul(o_ps[(h % 2) * DH:(h % 2 + 1) * DH, w * W:(w + 1) * W],
                                               V[:, w, h * DH:(h + 1) * DH], PT[:, h % 2, w * W:(w + 1) * W],
                                               start=True, stop=True)
                    ins.then_inc(pv_done, 1)
                    if h % 2 == 1:
                        p = h // 2
                        pe.wait_ge(rinv_ready, p + 1)
                        pe.wait_ge(r_copied, p)
                        for q in range(NT):
                            for o in range(2):
                                ins = nc.tensor.matmul(m_ps[o * DH:(o + 1) * DH, 0, q * P:(q + 1) * P],
                                                       rinv[:, h - 1 + o, q:q + 1].broadcast_to([P, DH]),
                                                       ident[:], start=True, stop=True)
                        ins.then_inc(r_done, 1)
                pe.wait_ge(out_scaled, FPAIR)
                for q in range(NT):
                    for p in range(FPAIR):
                        ins = nc.tensor.matmul(m_ps[:, 1, q * P:(q + 1) * P], oT[:, p, q * P:(q + 1) * P],
                                               wo[:, p, :], start=(p == 0), stop=(p == FPAIR - 1))
                ins.then_inc(wo_done, 1)

            @block.scalar
            def _(act):
                act.wait_ge(h_turned, 1)
                nc.scalar.activation(hT[0:DH, W:W + S], m_ps[0:DH, 0, :], ACT.Copy).then_inc(hT_ready, 1)
                nc.scalar.activation(hT[DH:P, W + 1:W + S], m_ps[DH:P, 0, 0:S - 1], ACT.Copy)\
                    .then_inc(hT_ready, 1)
                for j in range(NT):
                    act.wait_ge(qk_done, j + 1)
                    act.wait_ge(ss_ready, j)
                    nc.scalar.activation(raw[:, j, :], qk_ps[:], ACT.Copy).then_inc(raw_ready, 1)
                    nc.scalar.activation(sq[:], qk_ps[:], ACT.Square).then_inc(sq_ready, 1)
                act.wait_ge(ss_ready, NT)
                nc.scalar.activation(rn[:], ss[:], ACT.Sqrt).then_inc(root_ready, 1)
                for w in range(NW):
                    act.wait_ge(v_done, w + 1)
                    nc.scalar.activation(V[:, w, :], m_ps[:, w % 2, :], ACT.Copy).then_inc(v_copied, 1)
                for j in range(NT):
                    act.wait_ge(qk_turned, 2 * j + 1)
                    nc.scalar.activation(qT[:, :, j * P:(j + 1) * P],
                                         m_ps[:, 0, :].rearrange("p (c t) -> p c t", c=FPAIR), ACT.Copy)\
                        .then_inc(qkT_ready, 1)
                    act.wait_ge(qk_turned, 2 * j + 2)
                    nc.scalar.activation(kT[:, :, W + j * P:W + (j + 1) * P],
                                         m_ps[:, 1, :].rearrange("p (c t) -> p c t", c=FPAIR), ACT.Copy)\
                        .then_inc(qkT_ready, 1)
                for h in range(FH):
                    act.wait_ge(biased_done, h + 1)
                    if h > 1:
                        act.wait_ge(p_turned, h - 1)
                    for u in range(NT):
                        ins = nc.scalar.activation(prob[:, h % 2, u * P:(u + 1) * P],
                                                   biased[:, h % 2, u * P:(u + 1) * P], ACT.Exp,
                                                   bias=negmax[:, h, u:u + 1], scale=-1.0,
                                                   accum_out=sums[:, h, u:u + 1])
                    ins.then_inc(exp_done, 1)
                    if h % 2 == 1:
                        p = h // 2
                        act.wait_ge(r_done, p + 1)
                        act.wait_ge(out_scaled, p)
                        nc.scalar.activation(Rs[:], m_ps[:, 0, :], ACT.Copy).then_inc(r_copied, 1)

            @block.vector
            def _(dve):
                for j in range(NT):
                    dve.wait_ge(sq_ready, j + 1)
                    nc.vector.tensor_reduce(ss[:, j, :], sq[:].rearrange("p (h d) -> p h d", d=DH), AX.X, ALU.add)\
                        .then_inc(ss_ready, 1)
                    if j >= 1:
                        dve.wait_ge(rot_done, j)
                    for s in range(2):
                        c = slice(s * FH * DH, (s + 1) * FH * DH)
                        r3 = raw[:, j, c].rearrange("p (h d) -> p h d", d=DH)
                        o3 = t2[:, c].rearrange("p (h d) -> p h d", d=DH)
                        for half in range(2):
                            a, z = half * (DH // 2), (1 - half) * (DH // 2)
                            ins = nc.vector.tensor_tensor(
                                o3[:, :, a:a + DH // 2], r3[:, :, z:z + DH // 2],
                                ropeS[:, j, s:s + 1, a:a + DH // 2].broadcast_to([P, FH, DH // 2]), ALU.mult)
                    ins.then_inc(t2_ready, 1)
                    dve.wait_ge(t2_ready, j + 1)
                    dve.wait_ge(t1_ready, j + 1)
                    nc.vector.tensor_tensor(raw[:, j, :], t1[:, j % 2, :], t2[:], ALU.add).then_inc(rot_done, 1)
                dve.wait_ge(root_ready, 1)
                nc.vector.tensor_scalar(rn[:], rn[:], 1e-12, None, ALU.max).then_inc(rn_ready, 1)
                dve.wait_ge(rn_ready, 1)
                nc.vector.reciprocal(rn[:], rn[:]).then_inc(rn_ready, 1)
                dve.wait_ge(rn_ready, 2)
                dve.wait_ge(rot_done, NT)
                for j in range(NT):
                    v = raw[:, j, :].rearrange("p (h d) -> p h d", d=DH)
                    nc.vector.tensor_tensor(v, v, rn[:, j, :].rearrange("p (h o) -> p h o", o=1)
                                            .broadcast_to([P, 2 * FH, DH]), ALU.mult).then_inc(qk_scaled, 1)

                def bias(h):
                    dve.wait_ge(score_done, h + 1)
                    if h > 1:
                        dve.wait_ge(exp_done, h - 1)
                    for u in range(NT):
                        ins = nc.vector.tensor_tensor_reduce(
                            out=biased[:, h % 2, u * P:(u + 1) * P], in0=s_ps[:, h % 2, u * P:(u + 1) * P],
                            in1=mask[:, min(u, 1), :], scale=-1.0, scalar=-LOW, op0=ALU.add, op1=ALU.min,
                            accum_out=negmax[:, h, u:u + 1])
                    ins.then_inc(biased_done, 1)

                bias(0)
                for h in range(FH):
                    if h + 1 < FH:
                        bias(h + 1)
                    dve.wait_ge(p_turned, h + 1)
                    if h > 1:
                        dve.wait_ge(pv_done, h - 1)
                    nc.vector.tensor_copy(PT[:, h % 2, :], pt_ps[:]).then_inc(pt_copied, 1)
                    if h % 2 == 1:
                        p = h // 2
                        dve.wait_ge(exp_done, h + 1)
                        nc.vector.reciprocal(rinv[:, h - 1:h + 1, :], sums[:, h - 1:h + 1, :])\
                            .then_inc(rinv_ready, 1)
                        dve.wait_ge(r_copied, p + 1)
                        dve.wait_ge(pv_done, h + 1)
                        nc.vector.tensor_tensor(oT[:, p, :], o_ps[:], Rs[:], ALU.mult).then_inc(out_scaled, 1)
                dve.wait_ge(wo_done, 1)
                dve.wait_ge(hs_ready, 1)
                mine = H[:, bass.ds(b * NT, NT), :]
                nc.vector.tensor_tensor(mine, m_ps[:, 1, :].rearrange("p (j d) -> p j d", j=NT), mine,
                                        ALU.add).then_inc(h_added, 1)
        for s in sems:
            nc.gpsimd.sem_clear(s)
        nc.all_engine_barrier()


def gated_mlp(nc, ctx, tag, H, XH, mean, rstd, ident, gb, w1, b1, w2, b2, ones):
    def sb(name, shape):
        return ctx.enter_context(nc.sbuf_tensor(tag + name, shape, F32))

    def ps(name, shape):
        return ctx.enter_context(nc.psum_tensor(tag + name, shape, F32))

    sems = []

    def sem(name):
        sems.append(ctx.enter_context(nc.semaphore(tag + name)))
        return sems[-1]

    NC = len(CH)
    xs = sb("xs", [P, NT, D])
    xnT = sb("xnT", [P, S])
    gate = sb("gate", [P, 2, S])
    hid = sb("hid", [P, NC, S])
    x_ps = ps("x_ps", [P, S])
    a_ps = ps("a_ps", [P, 2, S])
    g_ps = ps("g_ps", [P, 2, S])
    y_ps = ps("y_ps", [P, S])
    xs_ready = sem("xs_ready")
    x_turned = sem("x_turned")
    xn_ready = sem("xn_ready")
    up_done = sem("up_done")
    gate_ready = sem("gate_ready")
    hid_ready = sem("hid_ready")
    down_done = sem("down_done")
    h_added = sem("h_added")

    with nc.Fori(0, NB) as b:
        with nc.Block() as block:

            @block.tensor
            def _(pe):
                pe.wait_ge(xs_ready, 1)
                for j in range(NT):
                    ins = nc.tensor.transpose(x_ps[:, j * P:(j + 1) * P], xs[:, j, :], ident[:])
                ins.then_inc(x_turned, 1)
                pe.wait_ge(xn_ready, 1)
                for c, (at, m) in enumerate(CH):
                    if c > 1:
                        pe.wait_ge(hid_ready, c - 1)
                    nc.tensor.matmul(g_ps[0:m, c % 2, :], w1[:, HID + at:HID + at + m], xnT[:], start=True, stop=True)
                    nc.tensor.matmul(a_ps[0:m, c % 2, :], w1[:, at:at + m], xnT[:], start=True, stop=True)\
                        .then_inc(up_done, 1)
                pe.wait_ge(hid_ready, NC)
                for q in range(NT):
                    for c, (at, m) in enumerate(CH):
                        nc.tensor.matmul(y_ps[:, q * P:(q + 1) * P], hid[0:m, c, q * P:(q + 1) * P],
                                         w2[0:m, c, :], start=(c == 0), stop=False)
                    ins = nc.tensor.matmul(y_ps[:, q * P:(q + 1) * P], ones[0:1, :], b2[0:1, :],
                                           start=False, stop=True)
                ins.then_inc(down_done, 1)

            @block.scalar
            def _(act):
                act.wait_ge(x_turned, 1)
                nc.scalar.activation(xnT[:], x_ps[:], ACT.Identity, bias=gb[:, 1:2], scale=gb[:, 0:1])\
                    .then_inc(xn_ready, 1)
                for c, (at, m) in enumerate(CH):
                    act.wait_ge(up_done, c + 1)
                    if c > 1:
                        act.wait_ge(hid_ready, c - 1)
                    nc.scalar.activation(gate[0:m, c % 2, :], g_ps[0:m, c % 2, :], ACT.Gelu,
                                         bias=b1[0:m, NC + c:NC + c + 1]).then_inc(gate_ready, 1)

            @block.vector
            def _(dve):
                for j in range(NT):
                    t = b * NT + j
                    ins = nc.vector.tensor_scalar(xs[:, j, :], XH[:, bass.ds(t, 1), :], mean[:, bass.ds(t, 1)],
                                                  rstd[:, bass.ds(t, 1)], ALU.subtract, ALU.mult)
                ins.then_inc(xs_ready, 1)
                for c, (at, m) in enumerate(CH):
                    dve.wait_ge(gate_ready, c + 1)
                    nc.vector.scalar_tensor_tensor(hid[0:m, c, :], a_ps[0:m, c % 2, :], b1[0:m, c:c + 1],
                                                   gate[0:m, c % 2, :], ALU.add, ALU.mult).then_inc(hid_ready, 1)
                dve.wait_ge(down_done, 1)
                mine = H[:, bass.ds(b * NT, NT), :]
                nc.vector.tensor_tensor(mine, y_ps[:].rearrange("p (j d) -> p j d", j=NT), mine,
                                        ALU.add).then_inc(h_added, 1)
        for s in sems:
            nc.gpsimd.sem_clear(s)
        nc.all_engine_barrier()


def build(nc, x, gamma, beta, Wq, Wk, Wv, Wo, wqkv, q_scale, k_scale, wo, ln_g, ln_b, w1, b1, w2, b2,
          c_ident, c_dist, c_mask, c_rope, out):
    NC = len(CH)
    ctx = ExitStack()
    with ctx:
        def sb(name, shape, c=ctx):
            return c.enter_context(nc.sbuf_tensor(name, shape, F32))

        X = sb("X", [P, TILES, D])
        ident = sb("ident", [P, P])
        mean = sb("mean", [P, TILES])
        rstd = sb("rstd", [P, TILES])
        work = (sb("bn", [P, TILES, 6]), sb("mv", [P, TILES, 2]), sb("root", [P, TILES]), sb("fac", [P, TILES]))
        loaded = ctx.enter_context(nc.semaphore("loaded"))
        x_dram = x.rearrange("b (j p) d -> p (b j) d", p=P)
        out_dram = out.rearrange("b (j p) d -> p (b j) d", p=P)

        with ExitStack() as c1:
            dist = sb("dist", [P, DW], c1)
            gb = sb("gb", [P, 2], c1)
            wqkv1 = sb("wqkv1", [P, 3 * NH * DH], c1)
            wo1 = sb("wo1", [P, NPAIR, D], c1)
            with nc.Block() as block:
                @block.sync
                def _(sp):
                    loads = [(X[:, 16 * i:16 * i + 16, :], x_dram[:, 16 * i:16 * i + 16, :]) for i in range(4)]
                    loads += [(ident[:], c_ident), (dist[:], c_dist),
                              (gb[:, 0:1], gamma.rearrange("(p o) -> p o", o=1)),
                              (gb[:, 1:2], beta.rearrange("(p o) -> p o", o=1)),
                              (wqkv1[:, 0:1024], Wq), (wqkv1[:, 1024:2048], Wk), (wqkv1[:, 2048:3072], Wv),
                              (wo1[:], Wo.rearrange("(c p) d -> p c d", p=P))]
                    for to, of in loads:
                        sp.dma_start(to, of).then_inc(loaded, 16)
                    sp.wait_ge(loaded, 16 * len(loads))
            layer_stats(nc, c1, "ln1", X, mean, rstd, work, True)
            global_attention(nc, c1, X, mean, rstd, ident, dist, gb, wqkv1, wo1)

        with ExitStack() as c2:
            H = sb("H", [P, TILES, D], c2)
            XH = sb("XH", [P, TILES, D], c2)
            normed = c2.enter_context(nc.semaphore("normed"))
            layer_stats(nc, c2, "ln2", X, mean, rstd, work, False)
            with nc.Block() as block:
                @block.vector
                def _(dve):
                    for t in range(TILES):
                        ins = nc.vector.tensor_scalar(H[:, t, :], X[:, t, :], mean[:, t:t + 1], rstd[:, t:t + 1],
                                                      ALU.subtract, ALU.mult)
                    ins.then_inc(normed, 1)
                    dve.wait_ge(normed, 1)
            for layer in range(DEPTH):
                tag = f"l{layer}_"
                with ExitStack() as c3:
                    mask = sb(tag + "mask", [P, 2, P], c3)
                    rope = sb(tag + "rope", [P, NT, 4, DH], c3)
                    scl = sb(tag + "scl", [P, 4, DH], c3)
                    wl = sb(tag + "wl", [P, 3 * S], c3)
                    wol = sb(tag + "wol", [P, FPAIR, D], c3)
                    ld = c3.enter_context(nc.semaphore(tag + "ld"))
                    rope_ready = c3.enter_context(nc.semaphore(tag + "rope_ready"))
                    with nc.Block() as block:
                        @block.sync
                        def _(sp):
                            loads = [(mask[:], c_mask), (rope[:], c_rope), (wl[:], wqkv[layer]),
                                     (wol[:], wo[layer].rearrange("(c p) d -> p c d", p=P))]
                            HF = DH // 2
                            for n, v in enumerate((q_scale, k_scale)):
                                row = v[layer:layer + 1, :]
                                loads += [(scl[:, n, :], row.broadcast_to([P, DH])),
                                          (scl[:, 2 + n, 0:HF], row[:, HF:DH].broadcast_to([P, HF])),
                                          (scl[:, 2 + n, HF:DH], row[:, 0:HF].broadcast_to([P, HF]))]
                            for to, of in loads:
                                sp.dma_start(to, of).then_inc(ld, 16)

                        @block.vector
                        def _(dve):
                            dve.wait_ge(ld, 16 * 10)
                            for j in range(NT):
                                ins = nc.vector.tensor_tensor(rope[:, j, :, :], rope[:, j, :, :], scl[:], ALU.mult)
                            ins.then_inc(rope_ready, 1)
                            dve.wait_ge(rope_ready, 1)
                    local_attention(nc, c3, tag, H, ident, mask, rope[:, :, 0:2, :], rope[:, :, 2:4, :], wl, wol)
                with ExitStack() as c4:
                    gbl = sb(tag + "gbl", [P, 2], c4)
                    w1l = sb(tag + "w1l", [P, 2 * HID], c4)
                    b1l = sb(tag + "b1l", [P, 2 * NC], c4)
                    w2l = sb(tag + "w2l", [P, NC, D], c4)
                    b2l = sb(tag + "b2l", [1, D], c4)
                    ones = sb(tag + "ones", [1, P], c4)
                    ld = c4.enter_context(nc.semaphore(tag + "ld2"))
                    filled = c4.enter_context(nc.semaphore(tag + "filled"))
                    copied = c4.enter_context(nc.semaphore(tag + "copied"))
                    with nc.Block() as block:
                        @block.sync
                        def _(sp):
                            g = "(p o) -> p o"
                            loads = [(gbl[:, 0:1], ln_g[layer].rearrange(g, o=1)),
                                     (gbl[:, 1:2], ln_b[layer].rearrange(g, o=1)),
                                     (w1l[:], w1[layer]), (b2l[:], b2[layer:layer + 1, :])]
                            for c, (at, m) in enumerate(CH):
                                loads += [(b1l[0:m, c:c + 1], b1[layer, at:at + m].rearrange(g, o=1)),
                                          (b1l[0:m, NC + c:NC + c + 1],
                                           b1[layer, HID + at:HID + at + m].rearrange(g, o=1)),
                                          (w2l[0:m, c, :], w2[layer, at:at + m, :])]
                            HF = D // 2
                            loads += [(XH[1:P, :, HF:D], H[0:P - 1, :, HF:D])]
                            early = XH[0:1, :, HF:D].rearrange("p (b j) d -> p b j d", j=NT)
                            late = H[P - 1:P, :, HF:D].rearrange("p (b j) d -> p b j d", j=NT)
                            loads += [(early[:, :, j, :], late[:, :, j - 1, :]) for j in range(1, NT)]
                            for to, of in loads:
                                sp.dma_start(to, of).then_inc(ld, 16)
                            sp.wait_ge(ld, 16 * len(loads))

                        @block.vector
                        def _(dve):
                            nc.vector.memset(XH[0:1, 0:TILES:NT, D // 2:D], 0.0)
                            nc.vector.memset(ones[:], 1.0)
                            nc.vector.tensor_copy(XH[:, :, 0:D // 2], H[:, :, 0:D // 2]).then_inc(filled, 1)
                            dve.wait_ge(filled, 1)
                    layer_stats(nc, c4, tag + "ln", XH, mean, rstd, work, False)
                    gated_mlp(nc, c4, tag, H, XH, mean, rstd, ident, gbl, w1l, b1l, w2l, b2l, ones)
            summed = c2.enter_context(nc.semaphore("summed"))
            stored = c2.enter_context(nc.semaphore("stored"))
            Q = TILES // 4
            with nc.Block() as block:
                @block.vector
                def _(dve):
                    for i in range(4):
                        s = slice(i * Q, (i + 1) * Q)
                        nc.vector.tensor_tensor(X[:, s, :], X[:, s, :], H[:, s, :], ALU.add).then_inc(summed, 1)

                @block.sync
                def _(sp):
                    for i in range(4):
                        s = slice(i * Q, (i + 1) * Q)
                        sp.wait_ge(summed, i + 1)
                        sp.dma_start(out_dram[:, s, :], X[:, s, :]).then_inc(stored, 16)
                    sp.wait_ge(stored, 64)


def constants():
    import numpy as np
    p = np.arange(P)
    ident = np.eye(P, dtype=np.float32)
    dist = np.abs(p[:, None] + (NT - 1) * P - np.arange(DW)[None, :]).astype(np.float32)
    i, j = (p % W)[:, None], np.arange(2 * W)[None, :]
    ok = (j <= i + W) & (j >= i)
    first = ok & ~((p[:, None] < W) & (j < W))
    mask = np.stack([np.where(first, 0, -1e30), np.where(ok, 0, -1e30)], 1).astype(np.float32)
    half = np.arange(0, DH, 2, dtype=np.float32)
    inv = (1.0 / 10000.0 ** (half / DH)).astype(np.float32)
    t = np.arange(S, dtype=np.float32)
    f = (t[:, None] * inv[None, :]).astype(np.float32)
    f = np.concatenate([f, f], -1)
    base = ((half + np.float32(0.4 * DH)) / np.float32(1.4 * DH)).astype(np.float32)
    power = (t - S // 2) / np.float32(W // 2)
    sc = (base[None, :] ** power[:, None]).astype(np.float32)
    sc = np.concatenate([sc, sc], -1)
    cos, sin = np.cos(f), np.sin(f)
    sin = np.concatenate([-sin[:, :DH // 2], sin[:, DH // 2:]], -1)
    rope = np.stack([8.0 * cos * sc, cos / sc, 8.0 * sin * sc, sin / sc], 1).astype(np.float32)
    rope = rope.reshape(NT, P, 4, DH).transpose(1, 0, 2, 3).copy()
    return {"c_ident": ident, "c_dist": dist, "c_mask": mask, "c_rope": rope}


_INS = ["L0_attn_x", "L0_attn_ln_gamma", "L0_attn_ln_beta", "L0_attn_Wq", "L0_attn_Wk", "L0_attn_Wv", "L0_attn_Wo",
        "L0_ffn_wqkv", "L0_ffn_q_scale", "L0_ffn_k_scale", "L0_ffn_wo", "L0_ffn_ln_g", "L0_ffn_ln_b", "L0_ffn_w1",
        "L0_ffn_b1", "L0_ffn_w2", "L0_ffn_b2"]


def kernel(**inputs):
    import numpy as _np
    import concourse.bacc as _bacc
    from concourse import mybir as _mybir
    from concourse.bass_utils import run_bass_kernel_spmd as _run

    nc = _bacc.Bacc("TRN2", target_bir_lowering=False, num_devices=1)
    arrays, args = {}, []
    given = [(n, _np.ascontiguousarray(inputs[n])) for n in _INS] + list(constants().items())
    for name, a in given:
        arrays[f"in_{name}_dram"] = a
        args.append(nc.dram_tensor(f"in_{name}_dram", a.shape, _mybir.dt.from_np(a.dtype), kind="ExternalInput").ap())
    args.append(nc.dram_tensor("out_0_dram", (NB, S, D), _mybir.dt.float32, kind="ExternalOutput").ap())
    build(nc, *args)
    r = _run(nc, [arrays], core_ids=[0])
    return r.results[0]["out_0_dram"]
```

```python
from contextlib import ExitStack

import concourse.bass as bass
from concourse import mybir

ALU = mybir.AluOpType
ACT = mybir.ActivationFunctionType
F32 = mybir.dt.float32
F32R = mybir.dt.float32r
AX = mybir.AxisListType

P = 128
NB, S, D = 16, 512, 128
NT = S // P
TILES = NB * NT
DH = 64
NH = 16
NPAIR = NH // 2
FH = 8
FPAIR = FH // 2
W = 64
NW = S // W
DEPTH = 2
HID = 341
DW = S + (NT - 1) * P
EPS = 1e-5
SCALE = float(DH) ** -0.5
CH = [(0, 128), (128, 128), (256, HID - 256)]
LOW = -3.0e38


def clear_counts(nc, sems):
    numbers = [s.num for s in sems]
    assert numbers == list(range(numbers[0], numbers[0] + len(numbers)))
    nc.gpsimd.sem_clear(range(numbers[0], numbers[0] + len(numbers)))
    nc.all_engine_barrier()


def layer_stats(nc, ctx, name, src, mean, rstd, work, twice):
    stats_done = ctx.enter_context(nc.semaphore(name + "_stats_done"))
    var_done = ctx.enter_context(nc.semaphore(name + "_var_done"))
    root_done = ctx.enter_context(nc.semaphore(name + "_root_done"))
    fac_done = ctx.enter_context(nc.semaphore(name + "_fac_done"))
    stats, mv, root, fac = work
    with nc.Block() as block:

        @block.vector
        def _(dve):
            for t in range(TILES):
                ins = nc.vector.bn_stats(stats[:, t, :], src[:, t, :])
            ins.then_inc(stats_done, 1)
            dve.wait_ge(stats_done, 1)
            for t in range(TILES):
                ins = nc.vector.bn_aggr(mv[:, t, :], stats[:, t, :])
            ins.then_inc(stats_done, 1)
            dve.wait_ge(stats_done, 2)
            nc.vector.tensor_copy(mean[:], mv[:, :, 0])
            nc.vector.tensor_scalar(fac[:], mv[:, :, 1], EPS, None, ALU.add).then_inc(var_done, 1)
            dve.wait_ge(root_done, 1)
            nc.vector.reciprocal(rstd[:], root[:]).then_inc(fac_done, 1)
            dve.wait_ge(fac_done, 1)
            if twice:
                nc.vector.tensor_tensor(fac[:], rstd[:], rstd[:], ALU.mult).then_inc(fac_done, 1)
                dve.wait_ge(fac_done, 2)
                nc.vector.tensor_tensor(fac[:], fac[:], mv[:, :, 1], ALU.mult).then_inc(fac_done, 1)
                dve.wait_ge(fac_done, 3)
                nc.vector.tensor_scalar(fac[:], fac[:], EPS, None, ALU.add).then_inc(var_done, 1)
                dve.wait_ge(root_done, 2)
                nc.vector.reciprocal(fac[:], root[:]).then_inc(fac_done, 1)
                dve.wait_ge(fac_done, 4)
                nc.vector.tensor_tensor(rstd[:], rstd[:], fac[:], ALU.mult).then_inc(fac_done, 1)

        @block.scalar
        def _(act):
            act.wait_ge(var_done, 1)
            nc.scalar.activation(root[:], fac[:], ACT.Sqrt).then_inc(root_done, 1)
            if twice:
                act.wait_ge(var_done, 2)
                nc.scalar.activation(root[:], fac[:], ACT.Sqrt).then_inc(root_done, 1)


def global_attention(nc, ctx, X, mean, rstd, ident, dist, gb, wqkv, wo):
    def sb(name, shape, dt=F32):
        return ctx.enter_context(nc.sbuf_tensor(name, shape, dt))

    def ps(name, shape):
        return ctx.enter_context(nc.psum_tensor(name, shape, F32))

    sems = []

    def sem(name):
        sems.append(ctx.enter_context(nc.semaphore(name)))
        return sems[-1]

    xs = sb("xs", [P, NT, D])
    xnT = sb("xnT", [P, 2, S])
    V = sb("V", [P, 2, NT, NH * DH])
    qs = sb("qs", [P, 2, 2, S], F32R)
    kh = sb("kh", [P, 2, 2, S], F32R)
    kl = sb("kl", [P, 2, 2, S], F32R)
    tab = sb("tab", [P, 4, DW])
    biased = sb("biased", [P, 2, S])
    negmax = sb("negmax", [P, NPAIR * 8])
    prob = sb("prob", [P, 2, 8, S])
    sums = sb("sums", [P, NPAIR, 2, NT])
    rinv = sb("rinv", [P, NPAIR, 2, NT])
    PT = sb("PT", [P, 2, 3, S])
    Rs = sb("Rs", [P, 2, S])
    oT = sb("oT", [P, NPAIR, S])
    PTN = 3

    sc_ps = ps("sc_ps", [P, 3, S])
    pt_ps = ps("pt_ps", [P, 2, S])
    o_ps = ps("o_ps", [P, S])
    m_ps = ps("m_ps", [P, 2, S])

    xs_ready = sem("xs_ready")
    xT_ready = sem("xT_ready")
    xn_ready = sem("xn_ready")
    v_done = sem("v_done")
    v_copied = sem("v_copied")
    q_done = sem("q_done")
    k_done = sem("k_done")
    q_high = sem("q_high")
    k_high = sem("k_high")
    q_low = sem("q_low")
    k_low = sem("k_low")
    tab_ready = sem("tab_ready")
    score_done = sem("score_done")
    biased_done = sem("biased_done")
    exp_done = sem("exp_done")
    turned = [sem("turned_a"), sem("turned_b")]
    pt_copied = [sem("pt_copied_act"), sem("pt_copied_dve")]
    pv_done = sem("pv_done")
    rinv_ready = sem("rinv_ready")
    r_done = sem("r_done")
    r_copied = sem("r_copied")
    out_scaled = sem("out_scaled")
    wo_done = sem("wo_done")
    x_added = sem("x_added")

    def clear():
        clear_counts(nc, sems)

    LO, HI = slice(0, DH), slice(DH, P)

    def f32(ap):
        return ap.bitcast(F32)


    def make_table(h):
        slope = 2.0 ** (-8.0 / (NH - h))
        nc.gpsimd.tensor_scalar(tab[:, h % 4, :], dist[:], -slope / SCALE, None, ALU.mult).then_inc(tab_ready, 1)

    def normalise(b):
        for j in range(NT):
            t = b * NT + j
            ins = nc.vector.tensor_scalar(xs[:, j, :], X[:, bass.ds(t, 1), :], mean[:, bass.ds(t, 1)],
                                          rstd[:, bass.ds(t, 1)], ALU.subtract, ALU.mult)
        ins.then_inc(xs_ready, 1)

    def turn_tokens(pe):
        pe.wait_ge(xs_ready, 1)
        for j in range(NT):
            ins = nc.tensor.transpose(m_ps[:, 0, j * P:(j + 1) * P], xs[:, j, :], ident[:])
        ins.then_inc(xT_ready, 1)

    def affine_tokens(act, seq):
        act.wait_ge(xT_ready, 1)
        nc.scalar.activation(xnT[:, seq, :], m_ps[:, 0, :], ACT.Identity, bias=gb[:, 1:2],
                             scale=gb[:, 0:1]).then_inc(xn_ready, 1)

    def project_values(seq, n, bank):
        j, half = n // 2, n % 2
        c = 2 * NH * DH + half * S
        nc.tensor.matmul(m_ps[:, bank, :], xnT[:, seq, j * P:(j + 1) * P], wqkv[:, c:c + S],
                         start=True, stop=True).then_inc(v_done, 1)

    def copy_values(act, seq, n, bank):
        j, half = n // 2, n % 2
        act.wait_ge(v_done, n + 1)
        nc.scalar.activation(V[:, seq, j, half * S:(half + 1) * S], m_ps[:, bank, :], ACT.Copy)\
            .then_inc(v_copied, 1)

    def project_queries(seq, p):
        nc.tensor.matmul(m_ps[:, 0, :], wqkv[:, p * P:(p + 1) * P], xnT[:, seq, :],
                         start=True, stop=True).then_inc(q_done, 1)

    def project_keys(seq, p):
        nc.tensor.matmul(m_ps[:, 1, :], wqkv[:, NH * DH + p * P:NH * DH + (p + 1) * P], xnT[:, seq, :],
                         start=True, stop=True).then_inc(k_done, 1)

    def query_high(par, h):
        rows = HI if h else LO
        nc.scalar.activation(qs[rows, par, h, :], m_ps[rows, 0, :], ACT.Copy).then_inc(q_high, 1)

    def query_low(par, h):
        rows, other = (HI, LO) if h else (LO, HI)
        nc.vector.tensor_tensor(qs[other, par, h, :], m_ps[rows, 0, :], f32(qs[rows, par, h, :]), ALU.subtract)\
            .then_inc(q_low, 1)

    def key_high(par, h, to):
        nc.scalar.activation(kh[to, par, h, :], m_ps[HI if h else LO, 1, :], ACT.Copy).then_inc(k_high, 1)

    def key_low(par, h, to):
        rows = HI if h else LO
        nc.vector.tensor_tensor(kl[to, par, h, :], m_ps[rows, 1, :], f32(kh[rows, par, h, :]), ALU.subtract)\
            .then_inc(k_low, 1)

    def score(par, n):
        h, q = n % 8 // NT, n % NT
        qb = qs[:, par, h, q * P:(q + 1) * P]
        nc.tensor.matmul(sc_ps[:, n % 3, :], qb, kh[:, par, h, :], start=True, stop=False)
        nc.tensor.matmul(sc_ps[:, n % 3, :], qb, kl[:, par, h, :], start=False, stop=True).then_inc(score_done, 1)

    def bias_scores(head, n):
        q = n % NT
        c = (NT - 1 - q) * P
        nc.vector.tensor_tensor_reduce(
            out=biased[:, n % 2, :], in0=sc_ps[:, n % 3, :], in1=tab[:, head % 4, c:c + S],
            scale=-SCALE, scalar=-LOW, op0=ALU.add, op1=ALU.min,
            accum_out=negmax[:, n:n + 1]).then_inc(biased_done, 1)

    def exponential(pair, n):
        i = n % 8
        nc.scalar.activation(prob[:, pair % 2, i, :], biased[:, n % 2, :], ACT.Exp, bias=negmax[:, n:n + 1],
                             scale=-1.0, accum_out=sums[:, pair, i // NT, i % NT:i % NT + 1]).then_inc(exp_done, 1)

    with nc.Block() as block:

        @block.gpsimd
        def _(pool):
            make_table(0)
            make_table(1)

        @block.tensor
        def _(pe):
            turn_tokens(pe)
            pe.wait_ge(xn_ready, 1)
            for n in range(2 * NT):
                if n:
                    pe.wait_ge(v_copied, n)
                project_values(0, n, 1)
            for p in range(2):
                pe.wait_ge(v_copied, 2 * NT)
                if p:
                    pe.wait_ge(q_low, 2 * p)
                    pe.wait_ge(k_low, 4 * p)
                project_queries(0, p)
                project_keys(0, p)
            for n in range(8):
                pe.wait_ge(q_low, 2)
                pe.wait_ge(k_low, 4)
                if n >= 3:
                    pe.wait_ge(biased_done, n - 2)
                score(0, n)

        @block.scalar
        def _(act):
            affine_tokens(act, 0)
            for n in range(2 * NT):
                copy_values(act, 0, n, 1)
            for p in range(2):
                act.wait_ge(q_done, p + 1)
                query_high(p, 0)
                query_high(p, 1)
                act.wait_ge(k_done, p + 1)
                for h in range(2):
                    key_high(p, h, LO)
                    key_high(p, h, HI)
            for n in range(8):
                act.wait_ge(biased_done, n + 1)
                exponential(0, n)

        @block.vector
        def _(dve):
            normalise(0)
            for p in range(2):
                dve.wait_ge(q_high, 2 * p + 2)
                query_low(p, 0)
                query_low(p, 1)
                dve.wait_ge(k_high, 4 * p + 4)
                for h in range(2):
                    key_low(p, h, LO)
                    key_low(p, h, HI)
            for n in range(8):
                dve.wait_ge(score_done, n + 1)
                if n % NT == 0:
                    dve.wait_ge(tab_ready, n // NT + 1)
                if n >= 2:
                    dve.wait_ge(exp_done, n - 1)
                bias_scores(n // NT, n)

    clear()

    def step(b, seq, more):
        with nc.Block() as block:

            def ahead(p, by):
                if p + by < NPAIR:
                    return seq, p + by
                return (1 - seq, p + by - NPAIR) if more else None

            @block.gpsimd
            def _(pool):
                for n in range(2 * NPAIR):
                    if n // 2 == NPAIR - 1 and not more:
                        continue
                    if n >= 4:
                        pool.wait_ge(biased_done, NT * (n - 3))
                    make_table((n + 2) % NH)

            @block.tensor
            def _(pe):
                def turn(p, i):
                    k, h = i // 2, i % 2
                    n = p * NT + k
                    if k == 0 and p >= 1:
                        pe.wait_ge(exp_done, (p - 1) * 8 + 4 * h + 4)
                    if n >= 1:
                        pe.wait_ge(pt_copied[h], n)
                    for q in range(NT):
                        ins = nc.tensor.transpose(pt_ps[:, h, q * P:(q + 1) * P],
                                                  prob[:, p % 2, 4 * h + q, k * P:(k + 1) * P], ident[:])
                    ins.then_inc(turned[h], 1)

                def mix(p, k):
                    n = p * NT + k
                    pe.wait_ge(pt_copied[0], n + 1)
                    pe.wait_ge(pt_copied[1], n + 1)
                    if k == 0 and p >= 1:
                        pe.wait_ge(out_scaled, p)
                    for h in range(2):
                        c = (2 * p + h) * DH
                        ins = nc.tensor.matmul(o_ps[h * DH:(h + 1) * DH, :], V[:, seq, k, c:c + DH],
                                               PT[:, h, n % PTN, :], start=(k == 0), stop=(k == NT - 1))
                    ins.then_inc(pv_done, 1)

                for p in range(NPAIR):
                    after, later = ahead(p, 1), ahead(p, 2)
                    for i in range(8):
                        n = p * 8 + i
                        if after:
                            if i % NT == 0 and p >= 1:
                                pe.wait_ge(q_low, 2 * p - 1 + i // NT)
                                pe.wait_ge(k_low, 4 * p - 2 + 2 * (i // NT))
                            if n >= 3:
                                pe.wait_ge(biased_done, n - 2)
                            score(after[1] % 2, n)
                        turn(p, i)
                        if i % 2 == 1 and i > 1:
                            mix(p, i // 2 - 1)
                        if i == 0 and later:
                            if p >= 1:
                                pe.wait_ge(r_copied, p)
                            if p + 2 >= NPAIR:
                                pe.wait_ge(xn_ready, 1)
                            project_queries(*later)
                        if i == 1 and p >= 1 and more:
                            pe.wait_ge(k_low, 4 * p)
                            pe.wait_ge(xn_ready, 1)
                            project_values(1 - seq, p - 1, 1)
                        if i == 2 and later:
                            if p >= 1:
                                pe.wait_ge(k_low, 4 * p)
                                if more:
                                    pe.wait_ge(v_copied, p)
                            project_keys(*later)
                        if i == 5 and more and p in (0, NPAIR - 1):
                            pe.wait_ge(q_low, 2 * p + 2)
                            if p == 0:
                                turn_tokens(pe)
                            else:
                                project_values(1 - seq, NPAIR - 1, 0)
                    pe.wait_ge(rinv_ready, p + 1)
                    if later:
                        pe.wait_ge(q_low, 2 * p + 2)
                    if p >= 1:
                        pe.wait_ge(r_copied, p)
                    if more and p == 0:
                        pe.wait_ge(xn_ready, 1)
                    if more and p == NPAIR - 1:
                        pe.wait_ge(v_copied, NPAIR)
                    for q in range(NT):
                        nc.tensor.transpose(m_ps[:, 0, q * P:(q + 1) * P],
                                            rinv[:, p, 1, q:q + 1].broadcast_to([P, P]), ident[:])
                        ins = nc.tensor.transpose(m_ps[LO, 0, q * P:(q + 1) * P],
                                                  rinv[:, p, 0, q:q + 1].broadcast_to([P, DH]), ident[:])
                    ins.then_inc(r_done, 1)
                    mix(p, NT - 1)
                pe.wait_ge(out_scaled, NPAIR)
                if more:
                    pe.wait_ge(k_low, 4 * NPAIR)
                for q in range(NT):
                    for p in range(NPAIR):
                        ins = nc.tensor.matmul(m_ps[:, 1, q * P:(q + 1) * P], oT[:, p, q * P:(q + 1) * P],
                                               wo[:, p, :], start=(p == 0), stop=(p == NPAIR - 1))
                ins.then_inc(wo_done, 1)

            @block.scalar
            def _(act):
                for p in range(NPAIR):
                    after, later = ahead(p, 1), ahead(p, 2)
                    for i in range(8):
                        n = p * 8 + i
                        if after:
                            act.wait_ge(biased_done, n + 1)
                            if i == 0 and p >= 1:
                                act.wait_ge(turned[0], p * NT)
                                act.wait_ge(turned[1], p * NT)
                            exponential(after[1], n)
                        if i % 2 == 0:
                            k = p * NT + i // 2
                            act.wait_ge(turned[0], k + 1)
                            if k >= PTN:
                                act.wait_ge(pv_done, k - PTN + 1)
                            nc.scalar.activation(PT[:, 0, k % PTN, :], pt_ps[:, 0, :], ACT.Copy)\
                                .then_inc(pt_copied[0], 1)
                        if i == 1 and p >= 1 and more:
                            copy_values(act, 1 - seq, p - 1, 1)
                        if later and i in (2, 3):
                            if i == 2:
                                if p >= 1:
                                    act.wait_ge(score_done, 8 * p)
                                act.wait_ge(q_done, p + 1)
                            query_high(p % 2, i - 2)
                        if later and i >= 4:
                            if i == 4:
                                act.wait_ge(k_done, p + 1)
                            key_high(p % 2, (i - 4) // 2, HI if i % 2 else LO)
                        if i == 6 and more and p == 0:
                            affine_tokens(act, 1 - seq)
                        if i == 6 and more and p == NPAIR - 1:
                            copy_values(act, 1 - seq, NPAIR - 1, 0)
                    act.wait_ge(r_done, p + 1)
                    if p >= 2:
                        act.wait_ge(out_scaled, p - 1)
                    nc.scalar.activation(Rs[:, p % 2, :], m_ps[:, 0, :], ACT.Copy).then_inc(r_copied, 1)

            @block.vector
            def _(dve):
                for p in range(NPAIR):
                    after, later = ahead(p, 1), ahead(p, 2)
                    if p >= 1:
                        dve.wait_ge(exp_done, 8 * p)
                    nc.vector.reciprocal(rinv[:, p, :, :], sums[:, p, :, :]).then_inc(rinv_ready, 1)
                    for i in range(8):
                        n = p * 8 + i
                        if after:
                            dve.wait_ge(score_done, n + 1)
                            if i % NT == 0:
                                dve.wait_ge(tab_ready, 2 * p + i // NT + 1)
                            if n >= 2:
                                dve.wait_ge(exp_done, n - 1)
                            bias_scores(2 * after[1] + i // NT, n)
                        if i % 2 == 1:
                            k = p * NT + i // 2
                            dve.wait_ge(turned[1], k + 1)
                            if k >= PTN:
                                dve.wait_ge(pv_done, k - PTN + 1)
                            nc.vector.tensor_copy(PT[:, 1, k % PTN, :], pt_ps[:, 1, :]).then_inc(pt_copied[1], 1)
                        if more and p == 0 and i == 2:
                            normalise(b + 1)
                        if later and i in (3, 4):
                            dve.wait_ge(q_high, 2 * p + i - 2)
                            query_low(p % 2, i - 3)
                        if later and i == 6:
                            dve.wait_ge(k_high, 4 * p + 2)
                            key_low(p % 2, 0, LO)
                            key_low(p % 2, 0, HI)
                    dve.wait_ge(r_copied, p + 1)
                    dve.wait_ge(pv_done, (p + 1) * NT)
                    nc.vector.tensor_tensor(oT[:, p, :], o_ps[:], Rs[:, p % 2, :], ALU.mult)\
                        .then_inc(out_scaled, 1)
                    if later:
                        dve.wait_ge(k_high, 4 * p + 4)
                        key_low(p % 2, 1, LO)
                        key_low(p % 2, 1, HI)
                dve.wait_ge(wo_done, 1)
                mine = X[:, bass.ds(b * NT, NT), :]
                nc.vector.tensor_tensor(mine, m_ps[:, 1, :].rearrange("p (j d) -> p j d", j=NT), mine,
                                        ALU.add).then_inc(x_added, 1)

        clear()

    with nc.Fori(0, NB - 2, 2) as b:
        step(b, 0, True)
        step(b + 1, 1, True)
    step(NB - 2, 0, True)
    step(NB - 1, 1, False)


def local_attention(nc, ctx, tag, H, ident, mask, ropeC, ropeS, wqkv, wo):
    def sb(name, shape):
        return ctx.enter_context(nc.sbuf_tensor(tag + name, shape, F32))

    def ps(name, shape):
        return ctx.enter_context(nc.psum_tensor(tag + name, shape, F32))

    sems = []

    def sem(name):
        sems.append(ctx.enter_context(nc.semaphore(tag + name)))
        return sems[-1]

    QK = 2 * FH * DH
    LO, HI = slice(0, DH), slice(DH, P)
    hs = sb("hs", [P, NT, D])
    hT = sb("hT", [P, W + S])
    V = sb("V", [P, 2, NW, FH * DH])
    raw = sb("raw", [P, NT, QK])
    sq = sb("sq", [P, QK])
    t2 = sb("t2", [P, 2, QK])
    ss = sb("ss", [P, NT, 2 * FH])
    rn = sb("rn", [P, NT, 2 * FH])
    qT = sb("qT", [P, 2, FPAIR, S])
    kT = sb("kT", [P, 2, FPAIR, W + S])
    biased = sb("biased", [P, 2, S])
    negmax = sb("negmax", [P, FH, NT])
    prob = sb("prob", [P, 2, 2, S])
    sums = sb("sums", [P, FH, NT])
    rinv = sb("rinv", [P, FH, NT])
    PT = sb("PT", [P, 2, S])
    Rs = sb("Rs", [P, S])
    oT = sb("oT", [P, FPAIR, S])

    qk_ps = ps("qk_ps", [P, 2, S])
    m_ps = ps("m_ps", [P, S])
    s_ps = ps("s_ps", [P, 2, S])
    pt_ps = ps("pt_ps", [P, 2, S])
    o_ps = ps("o_ps", [P, S])

    zeroed = ctx.enter_context(nc.semaphore(tag + "zeroed"))
    hs_ready = sem("hs_ready")
    h_turned = sem("h_turned")
    hT_ready = sem("hT_ready")
    v_done = sem("v_done")
    v_copied = sem("v_copied")
    qk_done = sem("qk_done")
    raw_ready = sem("raw_ready")
    sq_ready = sem("sq_ready")
    ss_ready = sem("ss_ready")
    root_ready = sem("root_ready")
    rn_ready = sem("rn_ready")
    cos_ready = sem("cos_ready")
    t2_ready = sem("t2_ready")
    rot_done = sem("rot_done")
    qk_scaled = sem("qk_scaled")
    qk_turned = sem("qk_turned")
    qkT_ready = sem("qkT_ready")
    score_done = sem("score_done")
    biased_done = sem("biased_done")
    exp_done = sem("exp_done")
    p_turned = sem("p_turned")
    pt_copied = sem("pt_copied")
    pv_done = sem("pv_done")
    rinv_ready = sem("rinv_ready")
    r_done = sem("r_done")
    r_copied = sem("r_copied")
    out_scaled = sem("out_scaled")
    wo_done = sem("wo_done")
    h_added = sem("h_added")

    with nc.Block() as block:
        @block.vector
        def _(dve):
            nc.vector.memset(hT[:], 0.0).then_inc(zeroed, 1)
            nc.vector.memset(kT[:, :, :, 0:W], 0.0).then_inc(zeroed, 1)
            dve.wait_ge(zeroed, 2)

    def heads(ap):
        return ap.rearrange("p (h d) -> p h d", d=DH)

    def step(b, seq, attend, more):
        new = 1 - seq
        with nc.Block() as block:

            @block.gpsimd
            def _(pool):
                if not more:
                    return
                nc.gpsimd.tensor_copy(hs[:], H[:, bass.ds((b + 1) * NT, NT), :]).then_inc(hs_ready, 1)
                for j in range(NT):
                    pool.wait_ge(raw_ready, j + 1)
                    pool.wait_ge(t2_ready, j + 1)
                    for s in range(2):
                        c = slice(s * FH * DH, (s + 1) * FH * DH)
                        ins = nc.gpsimd.tensor_tensor(heads(raw[:, j, c]), heads(raw[:, j, c]),
                                                      ropeC[:, j, s:s + 1, :].broadcast_to([P, FH, DH]), ALU.mult)
                    ins.then_inc(cos_ready, 1)
                    pool.wait_ge(cos_ready, j + 1)
                    nc.gpsimd.tensor_tensor(raw[:, j, :], raw[:, j, :], t2[:, j % 2, :], ALU.add).then_inc(rot_done, 1)

            @block.tensor
            def _(pe):
                def turn_tokens():
                    pe.wait_ge(hs_ready, 1)
                    for j in range(NT):
                        ins = nc.tensor.transpose(m_ps[:, j * P:(j + 1) * P], hs[:, j, :], ident[:])
                    ins.then_inc(h_turned, 1)

                def project(j):
                    if j == 0:
                        pe.wait_ge(hT_ready, 2)
                    else:
                        pe.wait_ge(raw_ready, j)
                        pe.wait_ge(sq_ready, j)
                    for s in range(2):
                        ins = nc.tensor.matmul(qk_ps[:, s, :], hT[:, W + j * P:W + (j + 1) * P],
                                               wqkv[:, s * S:(s + 1) * S], start=True, stop=True)
                    ins.then_inc(qk_done, 1)

                def values(*windows):
                    for w in windows:
                        if w == 0:
                            pe.wait_ge(raw_ready, NT)
                            pe.wait_ge(sq_ready, NT)
                        if w >= 2:
                            pe.wait_ge(v_copied, w - 1)
                        nc.tensor.matmul(qk_ps[:, w % 2, :], hT[:, w * W:w * W + P], wqkv[:, 2 * S:3 * S],
                                         start=True, stop=True).then_inc(v_done, 1)

                def turn_qk(j):
                    pe.wait_ge(qk_scaled, j + 1)
                    for s in range(2):
                        if j == 0:
                            pe.wait_ge(v_copied, NW)
                        else:
                            pe.wait_ge(qkT_ready, 2 * j - 1 + s)
                        for c in range(FPAIR):
                            ins = nc.tensor.transpose(qk_ps[:, s, c * P:(c + 1) * P],
                                                      raw[:, j, s * S + c * P:s * S + (c + 1) * P], ident[:])
                        ins.then_inc(qk_turned, 1)

                def scores(p, h):
                    n, r = 2 * p + h, HI if h else LO
                    if p >= 1:
                        pe.wait_ge(biased_done, n - 1)
                    for w in range(NW):
                        o = (w % 2) * W
                        ins = nc.tensor.matmul(s_ps[o:o + W, h, (w // 2) * P:(w // 2 + 1) * P],
                                               qT[r, seq, p, w * W:(w + 1) * W],
                                               kT[r, seq, p, w * W:w * W + P], start=True, stop=True)
                    ins.then_inc(score_done, 1)

                def turn(p, h):
                    n = 2 * p + h
                    pe.wait_ge(exp_done, n + 1)
                    if p >= 1:
                        pe.wait_ge(pt_copied, n - 1)
                    for u in range(NT):
                        ins = nc.tensor.transpose(pt_ps[:, h, u * P:(u + 1) * P],
                                                  prob[:, p % 2, h, u * P:(u + 1) * P], ident[:])
                    ins.then_inc(p_turned, 1)

                def mix(p):
                    pe.wait_ge(pt_copied, 2 * p + 2)
                    if p >= 1:
                        pe.wait_ge(out_scaled, p)
                    for w in range(NW):
                        for h in range(2):
                            c = (2 * p + h) * DH
                            ins = nc.tensor.matmul(o_ps[h * DH:(h + 1) * DH, w * W:(w + 1) * W],
                                                   V[:, seq, w, c:c + DH], PT[:, h, w * W:(w + 1) * W],
                                                   start=True, stop=True)
                    ins.then_inc(pv_done, 1)

                def spread(p):
                    pe.wait_ge(rinv_ready, p + 1)
                    if p >= 1:
                        pe.wait_ge(r_copied, p)
                    elif more:
                        pe.wait_ge(hT_ready, 2)
                    for q in range(NT):
                        nc.tensor.transpose(m_ps[:, q * P:(q + 1) * P],
                                            rinv[:, 2 * p + 1, q:q + 1].broadcast_to([P, P]), ident[:])
                        ins = nc.tensor.transpose(m_ps[LO, q * P:(q + 1) * P],
                                                  rinv[:, 2 * p, q:q + 1].broadcast_to([P, DH]), ident[:])
                    ins.then_inc(r_done, 1)

                if not attend:
                    turn_tokens()
                    for j in range(NT):
                        project(j)
                    values(*range(NW))
                    for j in range(NT):
                        turn_qk(j)
                    return
                scores(0, 0)
                if more:
                    turn_tokens()
                scores(0, 1)
                for p in range(FPAIR):
                    if more and p < 2:
                        project(2 * p)
                    if more and p == 2:
                        values(2, 3)
                    if more and p == 3:
                        values(6, 7)
                    if p + 1 < FPAIR:
                        scores(p + 1, 0)
                    turn(p, 0)
                    if more and p < 2:
                        project(2 * p + 1)
                    if more and p == 2:
                        values(4)
                    if more and p == 3:
                        turn_qk(0)
                    if p + 1 < FPAIR:
                        scores(p + 1, 1)
                    turn(p, 1)
                    if more and p == 1:
                        values(0, 1)
                    if more and p == 2:
                        values(5)
                    if more and p == 3:
                        turn_qk(1)
                    mix(p)
                    spread(p)
                if more:
                    turn_qk(2)
                    turn_qk(3)
                pe.wait_ge(out_scaled, FPAIR)
                pe.wait_ge(r_copied, FPAIR)
                for q in range(NT):
                    for p in range(FPAIR):
                        ins = nc.tensor.matmul(m_ps[:, q * P:(q + 1) * P], oT[:, p, q * P:(q + 1) * P],
                                               wo[:, p, :], start=(p == 0), stop=(p == FPAIR - 1))
                ins.then_inc(wo_done, 1)

            @block.scalar
            def _(act):
                def shift_tokens():
                    act.wait_ge(h_turned, 1)
                    nc.scalar.activation(hT[LO, W:W + S], m_ps[LO, :], ACT.Copy).then_inc(hT_ready, 1)
                    nc.scalar.activation(hT[HI, W + 1:W + S], m_ps[HI, 0:S - 1], ACT.Copy).then_inc(hT_ready, 1)

                def take(j):
                    act.wait_ge(qk_done, j + 1)
                    nc.scalar.activation(raw[:, j, :], qk_ps[:], ACT.Copy).then_inc(raw_ready, 1)
                    if j:
                        act.wait_ge(ss_ready, j)
                    nc.scalar.activation(sq[:], qk_ps[:], ACT.Square).then_inc(sq_ready, 1)

                def root():
                    act.wait_ge(ss_ready, NT)
                    nc.scalar.activation(rn[:], ss[:], ACT.Sqrt).then_inc(root_ready, 1)

                def values(*windows):
                    for w in windows:
                        act.wait_ge(v_done, w + 1)
                        nc.scalar.activation(V[:, new, w, :], qk_ps[:, w % 2, :], ACT.Copy).then_inc(v_copied, 1)

                def take_turned(j):
                    for s in range(2):
                        to = qT[:, new, :, j * P:(j + 1) * P] if s == 0 else \
                            kT[:, new, :, W + j * P:W + (j + 1) * P]
                        act.wait_ge(qk_turned, 2 * j + s + 1)
                        nc.scalar.activation(to, qk_ps[:, s, :].rearrange("p (c t) -> p c t", c=FPAIR), ACT.Copy)\
                            .then_inc(qkT_ready, 1)

                def exponential(p, h):
                    n = 2 * p + h
                    act.wait_ge(biased_done, n + 1)
                    if n >= 4:
                        act.wait_ge(p_turned, n - 3)
                    for u in range(NT):
                        ins = nc.scalar.activation(prob[:, p % 2, h, u * P:(u + 1) * P],
                                                   biased[:, h, u * P:(u + 1) * P], ACT.Exp,
                                                   bias=negmax[:, n, u:u + 1], scale=-1.0,
                                                   accum_out=sums[:, n, u:u + 1])
                    ins.then_inc(exp_done, 1)

                if not attend:
                    shift_tokens()
                    for j in range(NT):
                        take(j)
                    root()
                    values(*range(NW))
                    for j in range(NT):
                        take_turned(j)
                    return
                exponential(0, 0)
                if more:
                    shift_tokens()
                exponential(0, 1)
                for p in range(FPAIR):
                    if more and p < 2:
                        take(2 * p)
                    if more and p == 2:
                        root()
                        values(2, 3)
                    if more and p == 3:
                        values(6, 7)
                    if p + 1 < FPAIR:
                        exponential(p + 1, 0)
                    if more and p < 2:
                        take(2 * p + 1)
                    if more and p == 2:
                        values(4)
                    if more and p == 3:
                        take_turned(0)
                    if p + 1 < FPAIR:
                        exponential(p + 1, 1)
                    if more and p == 1:
                        values(0, 1)
                    if more and p == 2:
                        values(5)
                    if more and p == 3:
                        take_turned(1)
                    act.wait_ge(r_done, p + 1)
                    if p >= 1:
                        act.wait_ge(out_scaled, p)
                    nc.scalar.activation(Rs[:], m_ps[:], ACT.Copy).then_inc(r_copied, 1)
                if more:
                    take_turned(2)
                    take_turned(3)

            @block.vector
            def _(dve):
                def norms_and_sines(j):
                    dve.wait_ge(sq_ready, j + 1)
                    nc.vector.tensor_reduce(ss[:, j, :], heads(sq[:]), AX.X, ALU.add).then_inc(ss_ready, 1)
                    if j >= 2:
                        dve.wait_ge(rot_done, j - 1)
                    for s in range(2):
                        c = slice(s * FH * DH, (s + 1) * FH * DH)
                        r3, o3 = heads(raw[:, j, c]), heads(t2[:, j % 2, c])
                        for half in range(2):
                            a, z = half * (DH // 2), (1 - half) * (DH // 2)
                            ins = nc.vector.tensor_tensor(
                                o3[:, :, a:a + DH // 2], r3[:, :, z:z + DH // 2],
                                ropeS[:, j, s:s + 1, a:a + DH // 2].broadcast_to([P, FH, DH // 2]), ALU.mult)
                    ins.then_inc(t2_ready, 1)

                def inverse_norms():
                    dve.wait_ge(root_ready, 1)
                    nc.vector.tensor_scalar(rn[:], rn[:], 1e-12, None, ALU.max).then_inc(rn_ready, 1)
                    dve.wait_ge(rn_ready, 1)
                    nc.vector.reciprocal(rn[:], rn[:]).then_inc(rn_ready, 1)
                    dve.wait_ge(rn_ready, 2)

                def scale(j):
                    dve.wait_ge(rot_done, j + 1)
                    v = heads(raw[:, j, :])
                    nc.vector.tensor_tensor(v, v, rn[:, j, :].rearrange("p (h o) -> p h o", o=1)
                                            .broadcast_to([P, 2 * FH, DH]), ALU.mult).then_inc(qk_scaled, 1)

                def bias(p, h):
                    n = 2 * p + h
                    dve.wait_ge(score_done, n + 1)
                    if n >= 2:
                        dve.wait_ge(exp_done, n - 1)
                    for u in range(NT):
                        ins = nc.vector.tensor_tensor_reduce(
                            out=biased[:, h, u * P:(u + 1) * P], in0=s_ps[:, h, u * P:(u + 1) * P],
                            in1=mask[:, min(u, 1), :], scale=-1.0, scalar=-LOW, op0=ALU.add, op1=ALU.min,
                            accum_out=negmax[:, n, u:u + 1])
                    ins.then_inc(biased_done, 1)

                def take_turned(p, h):
                    n = 2 * p + h
                    dve.wait_ge(p_turned, n + 1)
                    if p >= 1:
                        dve.wait_ge(pv_done, p)
                    nc.vector.tensor_copy(PT[:, h, :], pt_ps[:, h, :]).then_inc(pt_copied, 1)

                if not attend:
                    for j in range(NT):
                        norms_and_sines(j)
                    inverse_norms()
                    for j in range(NT):
                        scale(j)
                    return
                bias(0, 0)
                bias(0, 1)
                for p in range(FPAIR):
                    if more and p == 2:
                        inverse_norms()
                    if more and p < 2:
                        norms_and_sines(2 * p)
                    if p + 1 < FPAIR:
                        bias(p + 1, 0)
                    take_turned(p, 0)
                    if more and p < 2:
                        norms_and_sines(2 * p + 1)
                    if more and p >= 2:
                        scale(2 * p - 4)
                    if p + 1 < FPAIR:
                        bias(p + 1, 1)
                    take_turned(p, 1)
                    nc.vector.reciprocal(rinv[:, 2 * p:2 * p + 2, :], sums[:, 2 * p:2 * p + 2, :])\
                        .then_inc(rinv_ready, 1)
                    if more and p >= 2:
                        scale(2 * p - 3)
                    dve.wait_ge(r_copied, p + 1)
                    dve.wait_ge(pv_done, p + 1)
                    nc.vector.tensor_tensor(oT[:, p, :], o_ps[:], Rs[:], ALU.mult).then_inc(out_scaled, 1)
                dve.wait_ge(wo_done, 1)
                mine = H[:, bass.ds(b * NT, NT), :]
                nc.vector.tensor_tensor(mine, m_ps[:].rearrange("p (j d) -> p j d", j=NT), mine,
                                        ALU.add).then_inc(h_added, 1)

        clear_counts(nc, sems)

    step(-1, 1, False, True)
    with nc.Fori(0, NB - 2, 2) as b:
        step(b, 0, True, True)
        step(b + 1, 1, True, True)
    step(NB - 2, 0, True, True)
    step(NB - 1, 1, True, False)


def gated_mlp(nc, ctx, tag, H, XH, mean, rstd, ident, gb, w1, b1, w2, b2, ones):
    def sb(name, shape):
        return ctx.enter_context(nc.sbuf_tensor(tag + name, shape, F32))

    def ps(name, shape):
        return ctx.enter_context(nc.psum_tensor(tag + name, shape, F32))

    sems = []

    def sem(name):
        sems.append(ctx.enter_context(nc.semaphore(tag + name)))
        return sems[-1]

    NC, G = len(CH), 4
    xs = sb("xs", [P, 2, NT, D])
    xnT = sb("xnT", [P, 2, S])
    gate = sb("gate", [P, 2, S])
    hid = sb("hid", [P, 2, NC, S])
    x_ps = ps("x_ps", [P, S])
    a_ps = ps("a_ps", [P, 2, S])
    g_ps = ps("g_ps", [P, 2, S])
    y_ps = ps("y_ps", [P, 2, S])
    xs_ready = sem("xs_ready")
    x_turned = sem("x_turned")
    xn_ready = sem("xn_ready")
    up_done = sem("up_done")
    gate_ready = sem("gate_ready")
    hid_ready = sem("hid_ready")
    down_done = sem("down_done")
    h_added = sem("h_added")

    with nc.Fori(0, NB - G + 1, G) as b:
        with nc.Block() as block:

            @block.tensor
            def _(pe):
                def up(g):
                    pe.wait_ge(xs_ready, g + 1)
                    if g >= 1:
                        pe.wait_ge(xn_ready, g)
                    for j in range(NT):
                        ins = nc.tensor.transpose(x_ps[:, j * P:(j + 1) * P], xs[:, g % 2, j, :], ident[:])
                    ins.then_inc(x_turned, 1)

                def hidden(g, c):
                    at, m = CH[c]
                    n = g * NC + c
                    if c == 0:
                        pe.wait_ge(xn_ready, g + 1)
                    if n >= 2:
                        pe.wait_ge(hid_ready, n - 1)
                    nc.tensor.matmul(g_ps[0:m, n % 2, :], w1[:, HID + at:HID + at + m], xnT[:, g % 2, :],
                                     start=True, stop=True)
                    nc.tensor.matmul(a_ps[0:m, n % 2, :], w1[:, at:at + m], xnT[:, g % 2, :],
                                     start=True, stop=True).then_inc(up_done, 1)

                def down(g):
                    pe.wait_ge(hid_ready, (g + 1) * NC)
                    if g >= 2:
                        pe.wait_ge(h_added, g - 1)
                    for q in range(NT):
                        to = y_ps[:, g % 2, q * P:(q + 1) * P]
                        for c, (at, m) in enumerate(CH):
                            nc.tensor.matmul(to, hid[0:m, g % 2, c, q * P:(q + 1) * P], w2[0:m, c, :],
                                             start=(c == 0), stop=False)
                        ins = nc.tensor.matmul(to, ones[0:1, :], b2[0:1, :], start=False, stop=True)
                    ins.then_inc(down_done, 1)

                up(0)
                for g in range(G):
                    for c in range(NC):
                        if c == 1 and g + 1 < G:
                            up(g + 1)
                        hidden(g, c)
                    if g >= 1:
                        down(g - 1)
                down(G - 1)

            @block.scalar
            def _(act):
                def affine(g):
                    act.wait_ge(x_turned, g + 1)
                    if g >= 2:
                        act.wait_ge(up_done, (g - 1) * NC)
                    nc.scalar.activation(xnT[:, g % 2, :], x_ps[:], ACT.Identity, bias=gb[:, 1:2],
                                         scale=gb[:, 0:1]).then_inc(xn_ready, 1)

                affine(0)
                for g in range(G):
                    for c, (at, m) in enumerate(CH):
                        n = g * NC + c
                        act.wait_ge(up_done, n + 1)
                        if n >= 2:
                            act.wait_ge(hid_ready, n - 1)
                        nc.scalar.activation(gate[0:m, n % 2, :], g_ps[0:m, n % 2, :], ACT.Gelu,
                                             bias=b1[0:m, NC + c:NC + c + 1]).then_inc(gate_ready, 1)
                        if c == 1 and g + 1 < G:
                            affine(g + 1)

            @block.vector
            def _(dve):
                def normalise(g):
                    if g >= 2:
                        dve.wait_ge(x_turned, g - 1)
                    for j in range(NT):
                        t = (b + g) * NT + j
                        ins = nc.vector.tensor_scalar(xs[:, g % 2, j, :], XH[:, bass.ds(t, 1), :],
                                                      mean[:, bass.ds(t, 1)], rstd[:, bass.ds(t, 1)],
                                                      ALU.subtract, ALU.mult)
                    ins.then_inc(xs_ready, 1)

                def add(g):
                    dve.wait_ge(down_done, g + 1)
                    mine = H[:, bass.ds((b + g) * NT, NT), :]
                    nc.vector.tensor_tensor(mine, y_ps[:, g % 2, :].rearrange("p (j d) -> p j d", j=NT), mine,
                                            ALU.add).then_inc(h_added, 1)

                normalise(0)
                normalise(1)
                for g in range(G):
                    for c, (at, m) in enumerate(CH):
                        n = g * NC + c
                        dve.wait_ge(gate_ready, n + 1)
                        if g >= 2 and c == 0:
                            dve.wait_ge(down_done, g - 1)
                        nc.vector.scalar_tensor_tensor(hid[0:m, g % 2, c, :], a_ps[0:m, n % 2, :], b1[0:m, c:c + 1],
                                                       gate[0:m, n % 2, :], ALU.add, ALU.mult).then_inc(hid_ready, 1)
                        if c == 0 and g >= 2:
                            add(g - 2)
                    if g + 2 < G:
                        normalise(g + 2)
                add(G - 2)
                add(G - 1)

        clear_counts(nc, sems)


def build(nc, x, gamma, beta, Wq, Wk, Wv, Wo, wqkv, q_scale, k_scale, wo, ln_g, ln_b, w1, b1, w2, b2,
          c_ident, c_dist, c_mask, c_rope, out):
    NC = len(CH)
    ctx = ExitStack()
    with ctx:
        def sb(name, shape, c=ctx):
            return c.enter_context(nc.sbuf_tensor(name, shape, F32))

        X = sb("X", [P, TILES, D])
        ident = sb("ident", [P, P])
        mean = sb("mean", [P, TILES])
        rstd = sb("rstd", [P, TILES])
        work = (sb("bn", [P, TILES, 6]), sb("mv", [P, TILES, 2]), sb("root", [P, TILES]), sb("fac", [P, TILES]))
        loaded = ctx.enter_context(nc.semaphore("loaded"))
        x_dram = x.rearrange("b (j p) d -> p (b j) d", p=P)
        out_dram = out.rearrange("b (j p) d -> p (b j) d", p=P)

        with ExitStack() as c1:
            dist = sb("dist", [P, DW], c1)
            gb = sb("gb", [P, 2], c1)
            wqkv1 = sb("wqkv1", [P, 3 * NH * DH], c1)
            wo1 = sb("wo1", [P, NPAIR, D], c1)
            with nc.Block() as block:
                @block.sync
                def _(sp):
                    loads = [(X[:, 16 * i:16 * i + 16, :], x_dram[:, 16 * i:16 * i + 16, :]) for i in range(4)]
                    loads += [(ident[:], c_ident), (dist[:], c_dist),
                              (gb[:, 0:1], gamma.rearrange("(p o) -> p o", o=1)),
                              (gb[:, 1:2], beta.rearrange("(p o) -> p o", o=1)),
                              (wqkv1[:, 0:1024], Wq), (wqkv1[:, 1024:2048], Wk), (wqkv1[:, 2048:3072], Wv),
                              (wo1[:], Wo.rearrange("(c p) d -> p c d", p=P))]
                    for to, of in loads:
                        sp.dma_start(to, of).then_inc(loaded, 16)
                    sp.wait_ge(loaded, 16 * len(loads))
            layer_stats(nc, c1, "ln1", X, mean, rstd, work, True)
            global_attention(nc, c1, X, mean, rstd, ident, dist, gb, wqkv1, wo1)

        with ExitStack() as c2:
            H = sb("H", [P, TILES, D], c2)
            normed = c2.enter_context(nc.semaphore("normed"))
            layer_stats(nc, c2, "ln2", X, mean, rstd, work, False)
            with nc.Block() as block:
                @block.vector
                def _(dve):
                    for t in range(TILES):
                        ins = nc.vector.tensor_scalar(H[:, t, :], X[:, t, :], mean[:, t:t + 1], rstd[:, t:t + 1],
                                                      ALU.subtract, ALU.mult)
                    ins.then_inc(normed, 1)
                    dve.wait_ge(normed, 1)
            for layer in range(DEPTH):
                tag = f"l{layer}_"
                with ExitStack() as c3:
                    mask = sb(tag + "mask", [P, 2, P], c3)
                    rope = sb(tag + "rope", [P, NT, 4, DH], c3)
                    scl = sb(tag + "scl", [P, 4, DH], c3)
                    wl = sb(tag + "wl", [P, 3 * S], c3)
                    wol = sb(tag + "wol", [P, FPAIR, D], c3)
                    ld = c3.enter_context(nc.semaphore(tag + "ld"))
                    rope_ready = c3.enter_context(nc.semaphore(tag + "rope_ready"))
                    with nc.Block() as block:
                        @block.sync
                        def _(sp):
                            loads = [(mask[:], c_mask), (rope[:], c_rope), (wl[:], wqkv[layer]),
                                     (wol[:], wo[layer].rearrange("(c p) d -> p c d", p=P))]
                            HF = DH // 2
                            for n, v in enumerate((q_scale, k_scale)):
                                row = v[layer:layer + 1, :]
                                loads += [(scl[:, n, :], row.broadcast_to([P, DH])),
                                          (scl[:, 2 + n, 0:HF], row[:, HF:DH].broadcast_to([P, HF])),
                                          (scl[:, 2 + n, HF:DH], row[:, 0:HF].broadcast_to([P, HF]))]
                            for to, of in loads:
                                sp.dma_start(to, of).then_inc(ld, 16)

                        @block.vector
                        def _(dve):
                            dve.wait_ge(ld, 16 * 10)
                            for j in range(NT):
                                ins = nc.vector.tensor_tensor(rope[:, j, :, :], rope[:, j, :, :], scl[:], ALU.mult)
                            ins.then_inc(rope_ready, 1)
                            dve.wait_ge(rope_ready, 1)
                    local_attention(nc, c3, tag, H, ident, mask, rope[:, :, 0:2, :], rope[:, :, 2:4, :], wl, wol)
                with ExitStack() as c4:
                    XH = sb(tag + "XH", [P, TILES, D], c4)
                    gbl = sb(tag + "gbl", [P, 2], c4)
                    w1l = sb(tag + "w1l", [P, 2 * HID], c4)
                    b1l = sb(tag + "b1l", [P, 2 * NC], c4)
                    w2l = sb(tag + "w2l", [P, NC, D], c4)
                    b2l = sb(tag + "b2l", [1, D], c4)
                    ones = sb(tag + "ones", [1, P], c4)
                    ld = c4.enter_context(nc.semaphore(tag + "ld2"))
                    filled = c4.enter_context(nc.semaphore(tag + "filled"))
                    copied = c4.enter_context(nc.semaphore(tag + "copied"))
                    with nc.Block() as block:
                        @block.sync
                        def _(sp):
                            g = "(p o) -> p o"
                            loads = [(gbl[:, 0:1], ln_g[layer].rearrange(g, o=1)),
                                     (gbl[:, 1:2], ln_b[layer].rearrange(g, o=1)),
                                     (w1l[:], w1[layer]), (b2l[:], b2[layer:layer + 1, :])]
                            for c, (at, m) in enumerate(CH):
                                loads += [(b1l[0:m, c:c + 1], b1[layer, at:at + m].rearrange(g, o=1)),
                                          (b1l[0:m, NC + c:NC + c + 1],
                                           b1[layer, HID + at:HID + at + m].rearrange(g, o=1)),
                                          (w2l[0:m, c, :], w2[layer, at:at + m, :])]
                            HF = D // 2
                            loads += [(XH[1:P, :, HF:D], H[0:P - 1, :, HF:D])]
                            early = XH[0:1, :, HF:D].rearrange("p (b j) d -> p b j d", j=NT)
                            late = H[P - 1:P, :, HF:D].rearrange("p (b j) d -> p b j d", j=NT)
                            loads += [(early[:, :, j, :], late[:, :, j - 1, :]) for j in range(1, NT)]
                            for to, of in loads:
                                sp.dma_start(to, of).then_inc(ld, 16)
                            sp.wait_ge(ld, 16 * len(loads))

                        @block.vector
                        def _(dve):
                            nc.vector.memset(XH[0:1, 0:TILES:NT, D // 2:D], 0.0)
                            nc.vector.memset(ones[:], 1.0)
                            nc.vector.tensor_copy(XH[:, :, 0:D // 2], H[:, :, 0:D // 2]).then_inc(filled, 1)
                            dve.wait_ge(filled, 1)
                    layer_stats(nc, c4, tag + "ln", XH, mean, rstd, work, False)
                    gated_mlp(nc, c4, tag, H, XH, mean, rstd, ident, gbl, w1l, b1l, w2l, b2l, ones)
            summed = c2.enter_context(nc.semaphore("summed"))
            stored = c2.enter_context(nc.semaphore("stored"))
            Q = TILES // 4
            with nc.Block() as block:
                @block.vector
                def _(dve):
                    for i in range(4):
                        s = slice(i * Q, (i + 1) * Q)
                        nc.vector.tensor_tensor(X[:, s, :], X[:, s, :], H[:, s, :], ALU.add).then_inc(summed, 1)

                @block.sync
                def _(sp):
                    for i in range(4):
                        s = slice(i * Q, (i + 1) * Q)
                        sp.wait_ge(summed, i + 1)
                        sp.dma_start(out_dram[:, s, :], X[:, s, :]).then_inc(stored, 16)
                    sp.wait_ge(stored, 64)


def constants():
    import numpy as np
    p = np.arange(P)
    ident = np.eye(P, dtype=np.float32)
    dist = np.abs(p[:, None] + (NT - 1) * P - np.arange(DW)[None, :]).astype(np.float32)
    i, j = (p % W)[:, None], np.arange(2 * W)[None, :]
    ok = (j <= i + W) & (j >= i)
    first = ok & ~((p[:, None] < W) & (j < W))
    mask = np.stack([np.where(first, 0, -1e30), np.where(ok, 0, -1e30)], 1).astype(np.float32)
    half = np.arange(0, DH, 2, dtype=np.float32)
    inv = (1.0 / 10000.0 ** (half / DH)).astype(np.float32)
    t = np.arange(S, dtype=np.float32)
    f = (t[:, None] * inv[None, :]).astype(np.float32)
    f = np.concatenate([f, f], -1)
    base = ((half + np.float32(0.4 * DH)) / np.float32(1.4 * DH)).astype(np.float32)
    power = (t - S // 2) / np.float32(W // 2)
    sc = (base[None, :] ** power[:, None]).astype(np.float32)
    sc = np.concatenate([sc, sc], -1)
    cos, sin = np.cos(f), np.sin(f)
    sin = np.concatenate([-sin[:, :DH // 2], sin[:, DH // 2:]], -1)
    rope = np.stack([8.0 * cos * sc, cos / sc, 8.0 * sin * sc, sin / sc], 1).astype(np.float32)
    rope = rope.reshape(NT, P, 4, DH).transpose(1, 0, 2, 3).copy()
    return {"c_ident": ident, "c_dist": dist, "c_mask": mask, "c_rope": rope}


_INS = ["L0_attn_x", "L0_attn_ln_gamma", "L0_attn_ln_beta", "L0_attn_Wq", "L0_attn_Wk", "L0_attn_Wv", "L0_attn_Wo",
        "L0_ffn_wqkv", "L0_ffn_q_scale", "L0_ffn_k_scale", "L0_ffn_wo", "L0_ffn_ln_g", "L0_ffn_ln_b", "L0_ffn_w1",
        "L0_ffn_b1", "L0_ffn_w2", "L0_ffn_b2"]


def kernel(**inputs):
    import numpy as _np
    import concourse.bacc as _bacc
    from concourse import mybir as _mybir
    from concourse.bass_utils import run_bass_kernel_spmd as _run

    nc = _bacc.Bacc("TRN2", target_bir_lowering=False, num_devices=1)
    arrays, args = {}, []
    given = [(n, _np.ascontiguousarray(inputs[n])) for n in _INS] + list(constants().items())
    for name, a in given:
        arrays[f"in_{name}_dram"] = a
        args.append(nc.dram_tensor(f"in_{name}_dram", a.shape, _mybir.dt.from_np(a.dtype), kind="ExternalInput").ap())
    args.append(nc.dram_tensor("out_0_dram", (NB, S, D), _mybir.dt.float32, kind="ExternalOutput").ap())
    build(nc, *args)
    r = _run(nc, [arrays], core_ids=[0])
    return r.results[0]["out_0_dram"]
```

```python
from contextlib import ExitStack

import concourse.bass as bass
from concourse import mybir

ALU = mybir.AluOpType
ACT = mybir.ActivationFunctionType
F32 = mybir.dt.float32
F32R = mybir.dt.float32r
AX = mybir.AxisListType

P = 128
NB, S, D = 16, 512, 128
NT = S // P
TILES = NB * NT
DH = 64
NH = 16
NPAIR = NH // 2
FH = 8
FPAIR = FH // 2
W = 64
NW = S // W
DEPTH = 2
HID = 341
DW = S + (NT - 1) * P
EPS = 1e-5
SCALE = float(DH) ** -0.5
CH = [(0, 128), (128, 128), (256, HID - 256)]
LOW = -3.0e38


def clear_counts(nc, sems):
    numbers = [s.num for s in sems]
    assert numbers == list(range(numbers[0], numbers[0] + len(numbers)))
    nc.gpsimd.sem_clear(range(numbers[0], numbers[0] + len(numbers)))
    nc.all_engine_barrier()


def layer_stats(nc, ctx, name, src, mean, rstd, twice, load=None, arrive=None):
    stats_done = ctx.enter_context(nc.semaphore(name + "_stats_done"))
    var_done = ctx.enter_context(nc.semaphore(name + "_var_done"))
    root_done = ctx.enter_context(nc.semaphore(name + "_root_done"))
    fac_done = ctx.enter_context(nc.semaphore(name + "_fac_done"))
    with ExitStack() as own, nc.Block() as block:
        stats, mv, root, fac = (own.enter_context(nc.sbuf_tensor(name + n, [P, TILES] + w, F32))
                                for n, w in (("_stats", [6]), ("_mv", [2]), ("_root", []), ("_fac", [])))

        if load:
            @block.sync
            def _(sp):
                load(sp)

        @block.vector
        def _(dve):
            for t in range(TILES):
                if arrive:
                    arrive(dve, t)
                ins = nc.vector.bn_stats(stats[:, t, :], src[:, t, :])
            ins.then_inc(stats_done, 1)
            dve.wait_ge(stats_done, 1)
            for t in range(TILES):
                ins = nc.vector.bn_aggr(mv[:, t, :], stats[:, t, :])
            ins.then_inc(stats_done, 1)
            dve.wait_ge(stats_done, 2)
            nc.vector.tensor_copy(mean[:], mv[:, :, 0])
            nc.vector.tensor_scalar(fac[:], mv[:, :, 1], EPS, None, ALU.add).then_inc(var_done, 1)
            dve.wait_ge(root_done, 1)
            nc.vector.reciprocal(rstd[:], root[:]).then_inc(fac_done, 1)
            dve.wait_ge(fac_done, 1)
            if twice:
                nc.vector.tensor_tensor(fac[:], rstd[:], rstd[:], ALU.mult).then_inc(fac_done, 1)
                dve.wait_ge(fac_done, 2)
                nc.vector.tensor_tensor(fac[:], fac[:], mv[:, :, 1], ALU.mult).then_inc(fac_done, 1)
                dve.wait_ge(fac_done, 3)
                nc.vector.tensor_scalar(fac[:], fac[:], EPS, None, ALU.add).then_inc(var_done, 1)
                dve.wait_ge(root_done, 2)
                nc.vector.reciprocal(fac[:], root[:]).then_inc(fac_done, 1)
                dve.wait_ge(fac_done, 4)
                nc.vector.tensor_tensor(rstd[:], rstd[:], fac[:], ALU.mult).then_inc(fac_done, 1)

        @block.scalar
        def _(act):
            act.wait_ge(var_done, 1)
            nc.scalar.activation(root[:], fac[:], ACT.Sqrt).then_inc(root_done, 1)
            if twice:
                act.wait_ge(var_done, 2)
                nc.scalar.activation(root[:], fac[:], ACT.Sqrt).then_inc(root_done, 1)


def global_attention(nc, ctx, X, mean, rstd, ident, dist, gb, wqkv, wo):
    def sb(name, shape, dt=F32):
        return ctx.enter_context(nc.sbuf_tensor(name, shape, dt))

    def ps(name, shape):
        return ctx.enter_context(nc.psum_tensor(name, shape, F32))

    sems = []

    def sem(name):
        sems.append(ctx.enter_context(nc.semaphore(name)))
        return sems[-1]

    xs = sb("xs", [P, NT, D])
    xnT = sb("xnT", [P, 2, S])
    V = sb("V", [P, 2, NT, NH * DH])
    qs = sb("qs", [P, 2, 2, S], F32R)
    kh = sb("kh", [P, 2, 2, S], F32R)
    kl = sb("kl", [P, 2, 2, S], F32R)
    tab = sb("tab", [P, 4, DW])
    biased = sb("biased", [P, 2, S])
    negmax = sb("negmax", [P, NPAIR * 8])
    prob = sb("prob", [P, 2, 8, S])
    sums = sb("sums", [P, NPAIR, 2, NT])
    rinv = sb("rinv", [P, NPAIR, 2, NT])
    PT = sb("PT", [P, 2, 3, S])
    Rs = sb("Rs", [P, 2, S])
    oT = sb("oT", [P, NPAIR, S])
    PTN = 3

    sc_ps = ps("sc_ps", [P, 3, S])
    pt_ps = ps("pt_ps", [P, 2, S])
    o_ps = ps("o_ps", [P, S])
    m_ps = ps("m_ps", [P, 2, S])

    xs_ready = sem("xs_ready")
    xT_ready = sem("xT_ready")
    xn_ready = sem("xn_ready")
    v_done = sem("v_done")
    v_copied = sem("v_copied")
    q_done = sem("q_done")
    k_done = sem("k_done")
    q_high = sem("q_high")
    k_high = sem("k_high")
    q_low = sem("q_low")
    k_low = sem("k_low")
    tab_ready = sem("tab_ready")
    score_done = sem("score_done")
    biased_done = sem("biased_done")
    exp_done = sem("exp_done")
    turned = [sem("turned_a"), sem("turned_b")]
    pt_copied = [sem("pt_copied_act"), sem("pt_copied_dve")]
    pv_done = sem("pv_done")
    rinv_ready = sem("rinv_ready")
    r_done = sem("r_done")
    r_copied = sem("r_copied")
    out_scaled = sem("out_scaled")
    wo_done = sem("wo_done")
    x_added = sem("x_added")

    def clear():
        clear_counts(nc, sems)

    LO, HI = slice(0, DH), slice(DH, P)

    def f32(ap):
        return ap.bitcast(F32)


    def make_table(h):
        slope = 2.0 ** (-8.0 / (NH - h))
        nc.gpsimd.tensor_scalar(tab[:, h % 4, :], dist[:], -slope / SCALE, None, ALU.mult).then_inc(tab_ready, 1)

    def normalise(b):
        for j in range(NT):
            t = b * NT + j
            ins = nc.vector.tensor_scalar(xs[:, j, :], X[:, bass.ds(t, 1), :], mean[:, bass.ds(t, 1)],
                                          rstd[:, bass.ds(t, 1)], ALU.subtract, ALU.mult)
        ins.then_inc(xs_ready, 1)

    def turn_tokens(pe):
        pe.wait_ge(xs_ready, 1)
        for j in range(NT):
            ins = nc.tensor.transpose(m_ps[:, 0, j * P:(j + 1) * P], xs[:, j, :], ident[:])
        ins.then_inc(xT_ready, 1)

    def affine_tokens(act, seq):
        act.wait_ge(xT_ready, 1)
        nc.scalar.activation(xnT[:, seq, :], m_ps[:, 0, :], ACT.Identity, bias=gb[:, 1:2],
                             scale=gb[:, 0:1]).then_inc(xn_ready, 1)

    def project_values(seq, n, bank):
        j, half = n // 2, n % 2
        c = 2 * NH * DH + half * S
        nc.tensor.matmul(m_ps[:, bank, :], xnT[:, seq, j * P:(j + 1) * P], wqkv[:, c:c + S],
                         start=True, stop=True).then_inc(v_done, 1)

    def copy_values(act, seq, n, bank):
        j, half = n // 2, n % 2
        act.wait_ge(v_done, n + 1)
        nc.scalar.activation(V[:, seq, j, half * S:(half + 1) * S], m_ps[:, bank, :], ACT.Copy)\
            .then_inc(v_copied, 1)

    def project_queries(seq, p):
        nc.tensor.matmul(m_ps[:, 0, :], wqkv[:, p * P:(p + 1) * P], xnT[:, seq, :],
                         start=True, stop=True).then_inc(q_done, 1)

    def project_keys(seq, p):
        nc.tensor.matmul(m_ps[:, 1, :], wqkv[:, NH * DH + p * P:NH * DH + (p + 1) * P], xnT[:, seq, :],
                         start=True, stop=True).then_inc(k_done, 1)

    def query_high(par, h):
        rows = HI if h else LO
        nc.scalar.activation(qs[rows, par, h, :], m_ps[rows, 0, :], ACT.Copy).then_inc(q_high, 1)

    def query_low(par, h):
        rows, other = (HI, LO) if h else (LO, HI)
        nc.vector.tensor_tensor(qs[other, par, h, :], m_ps[rows, 0, :], f32(qs[rows, par, h, :]), ALU.subtract)\
            .then_inc(q_low, 1)

    def key_high(par, h, to):
        nc.scalar.activation(kh[to, par, h, :], m_ps[HI if h else LO, 1, :], ACT.Copy).then_inc(k_high, 1)

    def key_low(par, h, to):
        rows = HI if h else LO
        nc.vector.tensor_tensor(kl[to, par, h, :], m_ps[rows, 1, :], f32(kh[rows, par, h, :]), ALU.subtract)\
            .then_inc(k_low, 1)

    def score(par, n):
        h, q = n % 8 // NT, n % NT
        qb = qs[:, par, h, q * P:(q + 1) * P]
        nc.tensor.matmul(sc_ps[:, n % 3, :], qb, kh[:, par, h, :], start=True, stop=False)
        nc.tensor.matmul(sc_ps[:, n % 3, :], qb, kl[:, par, h, :], start=False, stop=True).then_inc(score_done, 1)

    def bias_scores(head, n):
        q = n % NT
        c = (NT - 1 - q) * P
        nc.vector.tensor_tensor_reduce(
            out=biased[:, n % 2, :], in0=sc_ps[:, n % 3, :], in1=tab[:, head % 4, c:c + S],
            scale=-SCALE, scalar=-LOW, op0=ALU.add, op1=ALU.min,
            accum_out=negmax[:, n:n + 1]).then_inc(biased_done, 1)

    def exponential(pair, n):
        i = n % 8
        nc.scalar.activation(prob[:, pair % 2, i, :], biased[:, n % 2, :], ACT.Exp, bias=negmax[:, n:n + 1],
                             scale=-1.0, accum_out=sums[:, pair, i // NT, i % NT:i % NT + 1]).then_inc(exp_done, 1)

    with nc.Block() as block:

        @block.gpsimd
        def _(pool):
            for h in range(4):
                make_table(h)

        @block.tensor
        def _(pe):
            turn_tokens(pe)
            pe.wait_ge(xn_ready, 1)
            for n in range(2 * NT):
                if n:
                    pe.wait_ge(v_copied, n)
                project_values(0, n, 1)
            for p in range(2):
                pe.wait_ge(v_copied, 2 * NT)
                if p:
                    pe.wait_ge(q_low, 2 * p)
                    pe.wait_ge(k_low, 4 * p)
                project_queries(0, p)
                project_keys(0, p)
            for n in range(8):
                pe.wait_ge(q_low, 2)
                pe.wait_ge(k_low, 4)
                if n >= 3:
                    pe.wait_ge(biased_done, n - 2)
                score(0, n)

        @block.scalar
        def _(act):
            affine_tokens(act, 0)
            for n in range(2 * NT):
                copy_values(act, 0, n, 1)
            for p in range(2):
                act.wait_ge(q_done, p + 1)
                query_high(p, 0)
                query_high(p, 1)
                act.wait_ge(k_done, p + 1)
                for h in range(2):
                    key_high(p, h, LO)
                    key_high(p, h, HI)
            for n in range(8):
                act.wait_ge(biased_done, n + 1)
                exponential(0, n)

        @block.vector
        def _(dve):
            normalise(0)
            for p in range(2):
                dve.wait_ge(q_high, 2 * p + 2)
                query_low(p, 0)
                query_low(p, 1)
                dve.wait_ge(k_high, 4 * p + 4)
                for h in range(2):
                    key_low(p, h, LO)
                    key_low(p, h, HI)
            for n in range(8):
                dve.wait_ge(score_done, n + 1)
                if n % NT == 0:
                    dve.wait_ge(tab_ready, n // NT + 1)
                if n >= 2:
                    dve.wait_ge(exp_done, n - 1)
                bias_scores(n // NT, n)

    clear()

    def scale_pair(p):
        nc.vector.tensor_tensor(oT[:, p, :], o_ps[:], Rs[:, p % 2, :], ALU.mult).then_inc(out_scaled, 1)

    def project_out():
        for q in range(NT):
            for p in range(NPAIR):
                ins = nc.tensor.matmul(m_ps[:, 1, q * P:(q + 1) * P], oT[:, p, q * P:(q + 1) * P],
                                       wo[:, p, :], start=(p == 0), stop=(p == NPAIR - 1))
        ins.then_inc(wo_done, 1)

    def add_out(dve, b):
        dve.wait_ge(wo_done, 1)
        mine = X[:, bass.ds(b * NT, NT), :]
        nc.vector.tensor_tensor(mine, m_ps[:, 1, :].rearrange("p (j d) -> p j d", j=NT), mine,
                                ALU.add).then_inc(x_added, 1)

    def step(b, seq, more, last=True):
        scaled0, k_low0 = (1, 2) if last else (0, 0)
        with nc.Block() as block:

            def ahead(p, by):
                if p + by < NPAIR:
                    return seq, p + by
                return (1 - seq, p + by - NPAIR) if more else None

            @block.gpsimd
            def _(pool):
                for n in range(2 * NPAIR if more else 2 * NPAIR - 4):
                    if n >= 2:
                        pool.wait_ge(biased_done, NT * (n - 1))
                    make_table((n + 4) % NH)

            @block.tensor
            def _(pe):
                def turn(p, i):
                    k, h = i // 2, i % 2
                    n = p * NT + k
                    if k == 0 and p >= 1:
                        pe.wait_ge(exp_done, (p - 1) * 8 + 4 * h + 4)
                    if n >= 1:
                        pe.wait_ge(pt_copied[h], n)
                    for q in range(NT):
                        ins = nc.tensor.transpose(pt_ps[:, h, q * P:(q + 1) * P],
                                                  prob[:, p % 2, 4 * h + q, k * P:(k + 1) * P], ident[:])
                    ins.then_inc(turned[h], 1)

                def mix(p, k):
                    n = p * NT + k
                    pe.wait_ge(pt_copied[0], n + 1)
                    pe.wait_ge(pt_copied[1], n + 1)
                    if k == 0 and p + scaled0 >= 1:
                        pe.wait_ge(out_scaled, p + scaled0)
                    for h in range(2):
                        c = (2 * p + h) * DH
                        ins = nc.tensor.matmul(o_ps[h * DH:(h + 1) * DH, :], V[:, seq, k, c:c + DH],
                                               PT[:, h, n % PTN, :], start=(k == 0), stop=(k == NT - 1))
                    ins.then_inc(pv_done, 1)

                for p in range(NPAIR):
                    after, later = ahead(p, 1), ahead(p, 2)
                    for i in range(8):
                        n = p * 8 + i
                        if after:
                            if i % NT == 0 and p >= 1:
                                pe.wait_ge(q_low, 2 * p - 1 + i // NT)
                                pe.wait_ge(k_low, k_low0 + 4 * p - 2 + 2 * (i // NT))
                            elif i == NT and last:
                                pe.wait_ge(k_low, k_low0)
                            if n >= 3:
                                pe.wait_ge(biased_done, n - 2)
                            score(after[1] % 2, n)
                        turn(p, i)
                        if i % 2 == 1 and i > 1:
                            mix(p, i // 2 - 1)
                        if i == 0 and later:
                            if p >= 1:
                                pe.wait_ge(r_copied, p)
                            if p + 2 >= NPAIR:
                                pe.wait_ge(xn_ready, 1)
                            project_queries(*later)
                        if i == 1 and p == 0 and last:
                            pe.wait_ge(out_scaled, scaled0)
                            pe.wait_ge(k_low, k_low0)
                            project_out()
                        if i == 2 and p >= 1 and more:
                            pe.wait_ge(k_low, k_low0 + 4 * p)
                            pe.wait_ge(xn_ready, 1)
                            project_values(1 - seq, p - 1, 1)
                        if i == 4 and later:
                            if p == 0 and last:
                                pe.wait_ge(x_added, 1)
                            if p >= 1:
                                pe.wait_ge(k_low, k_low0 + 4 * p)
                                if more:
                                    pe.wait_ge(v_copied, p)
                            project_keys(*later)
                        if i == 5 and more and p in (0, NPAIR - 1):
                            pe.wait_ge(q_low, 2 * p + 2)
                            if p == 0:
                                turn_tokens(pe)
                            else:
                                project_values(1 - seq, NPAIR - 1, 0)
                    pe.wait_ge(rinv_ready, p + 1)
                    if later:
                        pe.wait_ge(q_low, 2 * p + 2)
                    if p >= 1:
                        pe.wait_ge(r_copied, p)
                    if more and p == 0:
                        pe.wait_ge(xn_ready, 1)
                    if more and p == NPAIR - 1:
                        pe.wait_ge(v_copied, NPAIR)
                    for q in range(NT):
                        nc.tensor.transpose(m_ps[:, 0, q * P:(q + 1) * P],
                                            rinv[:, p, 1, q:q + 1].broadcast_to([P, P]), ident[:])
                        ins = nc.tensor.transpose(m_ps[LO, 0, q * P:(q + 1) * P],
                                                  rinv[:, p, 0, q:q + 1].broadcast_to([P, DH]), ident[:])
                    ins.then_inc(r_done, 1)
                    mix(p, NT - 1)

            @block.scalar
            def _(act):
                for p in range(NPAIR):
                    after, later = ahead(p, 1), ahead(p, 2)
                    for i in range(8):
                        n = p * 8 + i
                        if after:
                            act.wait_ge(biased_done, n + 1)
                            if i == 0 and p >= 1:
                                act.wait_ge(turned[0], p * NT)
                                act.wait_ge(turned[1], p * NT)
                            exponential(after[1], n)
                        if i % 2 == 0:
                            k = p * NT + i // 2
                            act.wait_ge(turned[0], k + 1)
                            if k >= PTN:
                                act.wait_ge(pv_done, k - PTN + 1)
                            nc.scalar.activation(PT[:, 0, k % PTN, :], pt_ps[:, 0, :], ACT.Copy)\
                                .then_inc(pt_copied[0], 1)
                        if i == 2 and p >= 1 and more:
                            copy_values(act, 1 - seq, p - 1, 1)
                        if later and i in (2, 3):
                            if i == 2:
                                if p >= 1:
                                    act.wait_ge(score_done, 8 * p)
                                act.wait_ge(q_done, p + 1)
                            query_high(p % 2, i - 2)
                        if later and i >= 4:
                            if i == 4:
                                act.wait_ge(k_done, p + 1)
                            key_high(p % 2, (i - 4) // 2, HI if i % 2 else LO)
                        if i == 6 and more and p == 0:
                            affine_tokens(act, 1 - seq)
                        if i == 6 and more and p == NPAIR - 1:
                            copy_values(act, 1 - seq, NPAIR - 1, 0)
                    act.wait_ge(r_done, p + 1)
                    if p - 1 + scaled0 >= 1:
                        act.wait_ge(out_scaled, p - 1 + scaled0)
                    nc.scalar.activation(Rs[:, p % 2, :], m_ps[:, 0, :], ACT.Copy).then_inc(r_copied, 1)

            @block.vector
            def _(dve):
                def scale_mixed(p):
                    dve.wait_ge(r_copied, p + 1)
                    dve.wait_ge(pv_done, (p + 1) * NT)
                    scale_pair(p)

                def keys_low(p, h):
                    dve.wait_ge(k_high, 4 * p + 2 + 2 * h)
                    key_low(p % 2, h, LO)
                    key_low(p % 2, h, HI)

                for p in range(NPAIR):
                    after, later = ahead(p, 1), ahead(p, 2)
                    if p >= 1:
                        dve.wait_ge(exp_done, 8 * p)
                    nc.vector.reciprocal(rinv[:, p, :, :], sums[:, p, :, :]).then_inc(rinv_ready, 1)
                    for i in range(8):
                        n = p * 8 + i
                        if after:
                            dve.wait_ge(score_done, n + 1)
                            if i % NT == 0 and p >= 1:
                                dve.wait_ge(tab_ready, 2 * p + i // NT - 1)
                            if n >= 2:
                                dve.wait_ge(exp_done, n - 1)
                            bias_scores(2 * after[1] + i // NT, n)
                        if i == 0 and p == 0 and last:
                            scale_pair(NPAIR - 1)
                            for to in (LO, HI):
                                key_low((NPAIR - 1) % 2, 1, to)
                        if i == 0 and p >= 1:
                            scale_mixed(p - 1)
                            if ahead(p - 1, 2):
                                keys_low(p - 1, 1)
                        if i % 2 == 1:
                            k = p * NT + i // 2
                            dve.wait_ge(turned[1], k + 1)
                            if k >= PTN:
                                dve.wait_ge(pv_done, k - PTN + 1)
                            nc.vector.tensor_copy(PT[:, 1, k % PTN, :], pt_ps[:, 1, :]).then_inc(pt_copied[1], 1)
                        if last and p == 0 and i == 3:
                            add_out(dve, b - 1)
                        if more and p == 0 and i == 2:
                            normalise(b + 1)
                        if later and i in (3, 4):
                            dve.wait_ge(q_high, 2 * p + i - 2)
                            query_low(p % 2, i - 3)
                        if later and i == 7:
                            keys_low(p, 0)

        clear()

    step(0, 0, True, last=False)
    with nc.Fori(1, NB - 2, 2) as b:
        step(b, 1, True)
        step(b + 1, 0, True)
    step(NB - 1, 1, False)

    with nc.Block() as block:
        @block.tensor
        def _(pe):
            pe.wait_ge(out_scaled, 1)
            project_out()

        @block.vector
        def _(dve):
            scale_pair(NPAIR - 1)
            add_out(dve, NB - 1)


def local_attention(nc, ctx, tag, H, ident, mask, rope, scl, wqkv, wo):
    def sb(name, shape):
        return ctx.enter_context(nc.sbuf_tensor(tag + name, shape, F32))

    def ps(name, shape):
        return ctx.enter_context(nc.psum_tensor(tag + name, shape, F32))

    sems = []

    def sem(name):
        sems.append(ctx.enter_context(nc.semaphore(tag + name)))
        return sems[-1]

    QK = 2 * FH * DH
    ropeC, ropeS = rope[:, :, 0:2, :], rope[:, :, 2:4, :]
    LO, HI = slice(0, DH), slice(DH, P)
    hs = sb("hs", [P, 2, NT, D])
    hT = sb("hT", [P, S])
    V = sb("V", [P, 2, NT, FH * DH])
    V_even = sb("V_even", [P, 2, NT, FH * DH])
    raw = sb("raw", [P, NT, QK])
    sq = sb("sq", [P, QK])
    t2 = sb("t2", [P, 2, QK])
    rn = sb("rn", [P, NT, 2 * FH])
    qT = sb("qT", [P, 2, FPAIR, S])
    kT = sb("kT", [P, 2, FPAIR, 2, NT + 1, W])
    biased = sb("biased", [P, 2, S])
    negmax = sb("negmax", [P, FH, NT])
    prob = sb("prob", [P, 2, 2, S])
    sums = sb("sums", [P, FH, NT])
    rinv = sb("rinv", [P, FH, NT])
    PT = sb("PT", [P, 2, S])
    Rs = sb("Rs", [P, S])
    oT = sb("oT", [P, FPAIR, S])

    qk_ps = ps("qk_ps", [P, 2, S])
    m_ps = ps("m_ps", [P, S])
    s_ps = ps("s_ps", [P, 2, S])
    pt_ps = ps("pt_ps", [P, 2, S])
    o_ps = ps("o_ps", [P, S])

    zeroed = ctx.enter_context(nc.semaphore(tag + "zeroed"))
    hs_copied = sem("hs_copied")
    h_turned = sem("h_turned")
    hT_ready = sem("hT_ready")
    v_done = sem("v_done")
    v_copied = sem("v_copied")
    v_moved = sem("v_moved")
    qk_done = sem("qk_done")
    raw_ready = sem("raw_ready")
    sq_ready = sem("sq_ready")
    ss_ready = sem("ss_ready")
    root_ready = sem("root_ready")
    rn_ready = sem("rn_ready")
    cos_ready = sem("cos_ready")
    t2_ready = sem("t2_ready")
    rot_done = sem("rot_done")
    qk_scaled = sem("qk_scaled")
    qk_turned = sem("qk_turned")
    qkT_ready = sem("qkT_ready")
    score_done = sem("score_done")
    biased_done = sem("biased_done")
    exp_done = sem("exp_done")
    p_turned = sem("p_turned")
    pt_copied = sem("pt_copied")
    pv_done = sem("pv_done")
    rinv_ready = sem("rinv_ready")
    r_done = sem("r_done")
    r_copied = sem("r_copied")
    out_scaled = sem("out_scaled")
    wo_done = sem("wo_done")
    h_added = sem("h_added")
    wo_first_done = sem("wo_first_done")
    h_first_added = sem("h_first_added")

    with nc.Block() as block:
        @block.vector
        def _(dve):
            for j in range(NT):
                nc.vector.tensor_tensor(rope[:, j, :, :], rope[:, j, :, :], scl[:], ALU.mult).then_inc(zeroed, 1)
            nc.vector.memset(hT[:], 0.0).then_inc(zeroed, 1)
            nc.vector.memset(kT[:], 0.0).then_inc(zeroed, 1)
            nc.vector.memset(V_even[HI, :, 0, :], 0.0).then_inc(zeroed, 1)
            nc.vector.tensor_copy(hs[:], H[:, 0:2 * NT, :].rearrange("p (s j) d -> p s j d", s=2)).then_inc(zeroed, 1)
            dve.wait_ge(zeroed, 4 + NT)

    def heads(ap):
        return ap.rearrange("p (h d) -> p h d", d=DH)

    def window_keys(seq, p, r, w):
        flat = kT[r, seq, p].rearrange("p a u k -> p (a u k)")
        u = w // 2
        if w % 2:
            return flat.rearrange("p (a k) -> p a k", a=2)[:, :, u * W:(u + 1) * W]
        return flat[:, 0:2 * NT * W].rearrange("p (a k) -> p a k", a=2)[:, :, u * W:(u + 1) * W]

    def scale_pair(p):
        nc.vector.tensor_tensor(oT[:, p, :], o_ps[:], Rs[:], ALU.mult).then_inc(out_scaled, 1)

    def project_out(to, p, first, final):
        for j in range(NT):
            ins = nc.tensor.matmul(to[:, j * P:(j + 1) * P], oT[:, p, j * P:(j + 1) * P], wo[:, p, :],
                                   start=(p == first and j == 0), stop=(p == final and j == NT - 1))
        return ins

    def project_last():
        project_out(m_ps, FPAIR - 1, FPAIR - 1, FPAIR - 1).then_inc(wo_done, 1)

    def add_out(dve, b, of, done, added):
        dve.wait_ge(done, 1)
        mine = H[:, bass.ds(b * NT, NT), :]
        nc.vector.tensor_tensor(mine, of.rearrange("p (j d) -> p j d", j=NT), mine, ALU.add).then_inc(added, 1)

    def step(b, seq, attend, more, fetch=False, last=True):
        new = 1 - seq
        scaled0 = 1 if last else 0
        upcoming = [[(n // 2 + 1, n % 2)] for n in range(2 * FPAIR - 4)]
        upcoming += [[(FPAIR - 1, 0), (FPAIR - 1, 1)], [], [], []]
        with nc.Block() as block:

            @block.sync
            def _(sp):
                if not more:
                    return
                moved = 0
                for j in range(NT):
                    sp.wait_ge(v_copied, j + 1)
                    sp.dma_start(V_even[LO, new, j, :], V[LO, new, j, :]).then_inc(v_moved, 16)
                    moved += 16
                    if j + 1 < NT:
                        sp.dma_start(V_even[HI, new, j + 1, :], V[HI, new, j, :]).then_inc(v_moved, 16)
                        moved += 16
                sp.wait_ge(v_moved, moved)

            @block.gpsimd
            def _(pool):
                if not more:
                    return
                if fetch:
                    nc.gpsimd.tensor_copy(hs[:, seq], H[:, bass.ds((b + 2) * NT, NT), :]).then_inc(hs_copied, 1)
                for j in range(NT):
                    pool.wait_ge(raw_ready, j + 1)
                    pool.wait_ge(t2_ready, j + 1)
                    for s in range(2):
                        c = slice(s * FH * DH, (s + 1) * FH * DH)
                        ins = nc.gpsimd.tensor_tensor(heads(raw[:, j, c]), heads(raw[:, j, c]),
                                                      ropeC[:, j, s:s + 1, :].broadcast_to([P, FH, DH]), ALU.mult)
                    ins.then_inc(cos_ready, 1)
                    pool.wait_ge(cos_ready, j + 1)
                    nc.gpsimd.tensor_tensor(raw[:, j, :], raw[:, j, :], t2[:, j % 2, :], ALU.add).then_inc(rot_done, 1)

            @block.tensor
            def _(pe):
                def turn_tokens():
                    for j in range(NT):
                        ins = nc.tensor.transpose(m_ps[:, j * P:(j + 1) * P], hs[:, new, j, :], ident[:])
                    ins.then_inc(h_turned, 1)

                def project(j):
                    if j == 0:
                        pe.wait_ge(hT_ready, 2)
                    else:
                        pe.wait_ge(raw_ready, j)
                        pe.wait_ge(sq_ready, j)
                    for s in range(2):
                        ins = nc.tensor.matmul(qk_ps[:, s, :], hT[:, j * P:(j + 1) * P],
                                               wqkv[:, s * S:(s + 1) * S], start=True, stop=True)
                    ins.then_inc(qk_done, 1)

                def values(j):
                    if j == 0:
                        pe.wait_ge(raw_ready, NT)
                        pe.wait_ge(sq_ready, NT)
                    else:
                        pe.wait_ge(v_copied, j)
                        if j >= 3:
                            pe.wait_ge(qkT_ready, 2 * (j - 2))
                    nc.tensor.matmul(qk_ps[:, 1, :], hT[:, j * P:(j + 1) * P], wqkv[:, 2 * S:3 * S],
                                     start=True, stop=True).then_inc(v_done, 1)

                def turn_qk(j):
                    pe.wait_ge(qk_scaled, j + 1)
                    for s in range(2):
                        if s:
                            pe.wait_ge(v_copied, min(j + 3, NT))
                        if j >= 1:
                            pe.wait_ge(qkT_ready, 2 * j - 1 + s)
                        for c in range(FPAIR):
                            ins = nc.tensor.transpose(qk_ps[:, s, c * P:(c + 1) * P],
                                                      raw[:, j, s * S + c * P:s * S + (c + 1) * P], ident[:])
                        ins.then_inc(qk_turned, 1)

                def scores(p, h):
                    n, r = 2 * p + h, HI if h else LO
                    if p >= 1:
                        pe.wait_ge(biased_done, n - 1)
                    for w in range(NW):
                        o = (w % 2) * W
                        ins = nc.tensor.matmul(s_ps[o:o + W, h, (w // 2) * P:(w // 2 + 1) * P],
                                               qT[r, seq, p, w * W:(w + 1) * W],
                                               window_keys(seq, p, r, w), start=True, stop=True)
                    ins.then_inc(score_done, 1)

                def turn(p, h):
                    n = 2 * p + h
                    pe.wait_ge(exp_done, n + 1)
                    if p >= 1:
                        pe.wait_ge(pt_copied, n - 1)
                    for u in range(NT):
                        ins = nc.tensor.transpose(pt_ps[:, h, u * P:(u + 1) * P],
                                                  prob[:, p % 2, h, u * P:(u + 1) * P], ident[:])
                    ins.then_inc(p_turned, 1)

                def mix(p):
                    pe.wait_ge(pt_copied, 2 * p + 2)
                    if p + scaled0 >= 1:
                        pe.wait_ge(out_scaled, p + scaled0)
                    for w in range(NW):
                        of = V if w % 2 else V_even
                        for h in range(2):
                            c = (2 * p + h) * DH
                            ins = nc.tensor.matmul(o_ps[h * DH:(h + 1) * DH, w * W:(w + 1) * W],
                                                   of[:, seq, w // 2, c:c + DH], PT[:, h, w * W:(w + 1) * W],
                                                   start=True, stop=True)
                    ins.then_inc(pv_done, 1)

                def spread(p):
                    pe.wait_ge(rinv_ready, p + 1)
                    if p >= 1:
                        pe.wait_ge(r_copied, p)
                    elif last:
                        pe.wait_ge(h_added, 1)
                    elif more:
                        pe.wait_ge(hT_ready, 2)
                    for q in range(NT):
                        nc.tensor.transpose(m_ps[:, q * P:(q + 1) * P],
                                            rinv[:, 2 * p + 1, q:q + 1].broadcast_to([P, P]), ident[:])
                        ins = nc.tensor.transpose(m_ps[LO, q * P:(q + 1) * P],
                                                  rinv[:, 2 * p, q:q + 1].broadcast_to([P, DH]), ident[:])
                    ins.then_inc(r_done, 1)

                if not attend:
                    turn_tokens()
                    for j in range(NT):
                        project(j)
                    for j in range(NT + 2):
                        if j < NT:
                            values(j)
                        if j >= 2:
                            turn_qk(j - 2)
                    return
                if more:
                    turn_tokens()
                scores(0, 0)
                scores(0, 1)
                if more:
                    project(0)
                for p in range(FPAIR):
                    for h in range(2):
                        for ph in upcoming[2 * p + h]:
                            scores(*ph)
                        turn(p, h)
                        if p == 0 and h and last:
                            pe.wait_ge(out_scaled, scaled0)
                            if more:
                                pe.wait_ge(hT_ready, 2)
                            project_last()
                        if more and 2 * p + h + 1 < NT:
                            project(2 * p + h + 1)
                        if more and 0 <= 2 * p + h - 3 < NT:
                            values(2 * p + h - 3)
                        if 2 * p + h == 5:
                            pe.wait_ge(biased_done, 2 * FPAIR)
                            pe.wait_ge(out_scaled, scaled0 + 2)
                            project_out(s_ps[:, 0, :], 0, 0, 2)
                            project_out(s_ps[:, 0, :], 1, 0, 2)
                        if 2 * p + h == 7:
                            pe.wait_ge(out_scaled, scaled0 + 3)
                            project_out(s_ps[:, 0, :], 2, 0, 2).then_inc(wo_first_done, 1)
                        if h:
                            mix(p)
                            spread(p)
                        if more and 2 * p + h >= 5:
                            turn_qk(2 * p + h - 5)
                if more:
                    turn_qk(NT - 1)

            @block.scalar
            def _(act):
                def shift_tokens():
                    act.wait_ge(h_turned, 1)
                    nc.scalar.activation(hT[LO, :], m_ps[LO, :], ACT.Copy).then_inc(hT_ready, 1)
                    nc.scalar.activation(hT[HI, 1:S], m_ps[HI, 0:S - 1], ACT.Copy).then_inc(hT_ready, 1)

                def take(j):
                    act.wait_ge(qk_done, j + 1)
                    nc.scalar.activation(raw[:, j, :], qk_ps[:], ACT.Copy).then_inc(raw_ready, 1)
                    if j:
                        act.wait_ge(ss_ready, j)
                    nc.scalar.activation(sq[:], qk_ps[:], ACT.Square).then_inc(sq_ready, 1)

                def root():
                    act.wait_ge(ss_ready, NT)
                    nc.scalar.activation(rn[:], rn[:], ACT.Sqrt).then_inc(root_ready, 1)

                def values(j):
                    act.wait_ge(v_done, j + 1)
                    nc.scalar.activation(V[:, new, j, :], qk_ps[:, 1, :], ACT.Copy).then_inc(v_copied, 1)

                def take_turned(j):
                    for s in range(2):
                        act.wait_ge(qk_turned, 2 * j + s + 1)
                        if s == 0:
                            nc.scalar.activation(qT[:, new, :, j * P:(j + 1) * P],
                                                 qk_ps[:, 0, :].rearrange("p (c t) -> p c t", c=FPAIR), ACT.Copy)\
                                .then_inc(qkT_ready, 1)
                        else:
                            both = kT[:, new].rearrange("p c a u k -> p c (a u k)")\
                                .rearrange("p c (a k) -> p c a k", a=2)
                            nc.scalar.activation(both[:, :, :, j * W:(j + 1) * W],
                                                 qk_ps[:, 1, :].rearrange("p (c a k) -> p c a k", c=FPAIR, a=2),
                                                 ACT.Copy).then_inc(qkT_ready, 1)

                def exponential(p, h):
                    n = 2 * p + h
                    act.wait_ge(biased_done, n + 1)
                    if n >= 4:
                        act.wait_ge(p_turned, n - 3)
                    for u in range(NT):
                        ins = nc.scalar.activation(prob[:, p % 2, h, u * P:(u + 1) * P],
                                                   biased[:, h, u * P:(u + 1) * P], ACT.Exp,
                                                   bias=negmax[:, n, u:u + 1], scale=-1.0,
                                                   accum_out=sums[:, n, u:u + 1])
                    ins.then_inc(exp_done, 1)

                def spread_sums(p):
                    act.wait_ge(r_done, p + 1)
                    if p + scaled0 >= 1:
                        act.wait_ge(out_scaled, p + scaled0)
                    nc.scalar.activation(Rs[:], m_ps[:], ACT.Copy).then_inc(r_copied, 1)

                if not attend:
                    shift_tokens()
                    for j in range(NT):
                        take(j)
                    root()
                    for j in range(NT + 2):
                        if j < NT:
                            values(j)
                        if j >= 2:
                            take_turned(j - 2)
                    return
                if more:
                    shift_tokens()
                exponential(0, 0)
                if more:
                    take(0)
                exponential(0, 1)
                for p in range(FPAIR):
                    for h in range(2):
                        for ph in upcoming[2 * p + h][:1]:
                            exponential(*ph)
                        if more and 2 * p + h + 1 < NT:
                            take(2 * p + h + 1)
                        if more and 0 <= 2 * p + h - 3 < NT:
                            values(2 * p + h - 3)
                        for ph in upcoming[2 * p + h][1:]:
                            exponential(*ph)
                        if more and p == 2 and h == 0:
                            root()
                        if h:
                            spread_sums(p)
                        if more and 2 * p + h >= 5:
                            take_turned(2 * p + h - 5)
                if more:
                    take_turned(NT - 1)

            @block.vector
            def _(dve):
                def norms(j):
                    dve.wait_ge(sq_ready, j + 1)
                    nc.vector.tensor_reduce(rn[:, j, :], heads(sq[:]), AX.X, ALU.add).then_inc(ss_ready, 1)

                def sines(j):
                    dve.wait_ge(raw_ready, j + 1)
                    if j >= 2:
                        dve.wait_ge(rot_done, j - 1)
                    for s in range(2):
                        c = slice(s * FH * DH, (s + 1) * FH * DH)
                        r3, o3 = heads(raw[:, j, c]), heads(t2[:, j % 2, c])
                        for half in range(2):
                            a, z = half * (DH // 2), (1 - half) * (DH // 2)
                            ins = nc.vector.tensor_tensor(
                                o3[:, :, a:a + DH // 2], r3[:, :, z:z + DH // 2],
                                ropeS[:, j, s:s + 1, a:a + DH // 2].broadcast_to([P, FH, DH // 2]), ALU.mult)
                    ins.then_inc(t2_ready, 1)

                def inverse_norms():
                    dve.wait_ge(root_ready, 1)
                    nc.vector.tensor_scalar(rn[:], rn[:], 1e-12, None, ALU.max).then_inc(rn_ready, 1)
                    dve.wait_ge(rn_ready, 1)
                    nc.vector.reciprocal(rn[:], rn[:]).then_inc(rn_ready, 1)
                    dve.wait_ge(rn_ready, 2)

                def scale(j):
                    dve.wait_ge(rot_done, j + 1)
                    v = heads(raw[:, j, :])
                    nc.vector.tensor_tensor(v, v, rn[:, j, :].rearrange("p (h o) -> p h o", o=1)
                                            .broadcast_to([P, 2 * FH, DH]), ALU.mult).then_inc(qk_scaled, 1)

                def bias(p, h):
                    n = 2 * p + h
                    dve.wait_ge(score_done, n + 1)
                    if n >= 2:
                        dve.wait_ge(exp_done, n - 1)
                    for u in range(NT):
                        ins = nc.vector.tensor_tensor_reduce(
                            out=biased[:, h, u * P:(u + 1) * P], in0=s_ps[:, h, u * P:(u + 1) * P],
                            in1=mask[:, min(u, 1), :], scale=-1.0, scalar=-LOW, op0=ALU.add, op1=ALU.min,
                            accum_out=negmax[:, n, u:u + 1])
                    ins.then_inc(biased_done, 1)

                def take_turned(p, h):
                    n = 2 * p + h
                    dve.wait_ge(p_turned, n + 1)
                    if p >= 1:
                        dve.wait_ge(pv_done, p)
                    nc.vector.tensor_copy(PT[:, h, :], pt_ps[:, h, :]).then_inc(pt_copied, 1)

                def scale_mixed(p):
                    dve.wait_ge(r_copied, p + 1)
                    dve.wait_ge(pv_done, p + 1)
                    scale_pair(p)

                if not attend:
                    for j in range(NT):
                        sines(j)
                        norms(j)
                    inverse_norms()
                    for j in range(NT):
                        scale(j)
                    return
                if last:
                    scale_pair(FPAIR - 1)
                bias(0, 0)
                bias(0, 1)
                for p in range(FPAIR):
                    for h in range(2):
                        for ph in upcoming[2 * p + h]:
                            bias(*ph)
                        take_turned(p, h)
                        if h:
                            nc.vector.reciprocal(rinv[:, 2 * p:2 * p + 2, :], sums[:, 2 * p:2 * p + 2, :])\
                                .then_inc(rinv_ready, 1)
                        elif p >= 1:
                            scale_mixed(p - 1)
                        if last and h and p == 0:
                            add_out(dve, b - 1, m_ps[:], wo_done, h_added)
                        if more and 2 * p + h == NT + 1:
                            inverse_norms()
                        if more and p < 2:
                            norms(2 * p + h)
                        if more and p < 2:
                            sines(2 * p + h)
                        if more and 2 * p + h >= 5:
                            scale(2 * p + h - 5)
                if more:
                    scale(NT - 1)
                add_out(dve, b, s_ps[:, 0, :], wo_first_done, h_first_added)

        clear_counts(nc, sems)

    step(-1, 1, False, True)
    step(0, 0, True, True, fetch=True, last=False)
    with nc.Fori(1, NB - 4, 2) as b:
        step(b, 1, True, True, fetch=True)
        step(b + 1, 0, True, True, fetch=True)
    step(NB - 3, 1, True, True, fetch=True)
    step(NB - 2, 0, True, True)
    step(NB - 1, 1, True, False)

    with nc.Block() as block:
        @block.tensor
        def _(pe):
            pe.wait_ge(out_scaled, 1)
            project_last()

        @block.vector
        def _(dve):
            scale_pair(FPAIR - 1)
            add_out(dve, NB - 1, m_ps[:], wo_done, h_added)


def gated_mlp(nc, ctx, tag, H, XH, mean, rstd, ident, gb, w1, b1, w2, b2):
    def sb(name, shape):
        return ctx.enter_context(nc.sbuf_tensor(tag + name, shape, F32))

    def ps(name, shape):
        return ctx.enter_context(nc.psum_tensor(tag + name, shape, F32))

    sems = []

    def sem(name):
        sems.append(ctx.enter_context(nc.semaphore(tag + name)))
        return sems[-1]

    NC, G = len(CH), 8
    xs = sb("xs", [P, 2, NT, D])
    xnT = sb("xnT", [P, 2, S])
    gate = sb("gate", [P, 2, S])
    hid = sb("hid", [P, 2, NC, S])
    x_ps = ps("x_ps", [P, S])
    a_ps = ps("a_ps", [P, 2, S])
    g_ps = ps("g_ps", [P, 2, S])
    y_ps = ps("y_ps", [P, 2, S])
    xs_ready = sem("xs_ready")
    x_turned = sem("x_turned")
    xn_ready = sem("xn_ready")
    up_done = sem("up_done")
    gate_ready = sem("gate_ready")
    hid_ready = sem("hid_ready")
    down_done = sem("down_done")
    b2_added = sem("b2_added")
    h_added = sem("h_added")

    with nc.Fori(0, NB - G + 1, G) as b:
        with nc.Block() as block:

            @block.gpsimd
            def _(pool):
                for g in range(G):
                    mine = H[:, bass.ds((b + g) * NT, NT), :]
                    nc.gpsimd.tensor_tensor(mine, mine, b2[:].broadcast_to([P, NT, D]), ALU.add).then_inc(b2_added, 1)

            @block.tensor
            def _(pe):
                def up(g):
                    pe.wait_ge(xs_ready, g + 1)
                    if g >= 1:
                        pe.wait_ge(xn_ready, g)
                    for j in range(NT):
                        ins = nc.tensor.transpose(x_ps[:, j * P:(j + 1) * P], xs[:, g % 2, j, :], ident[:])
                    ins.then_inc(x_turned, 1)

                def hidden(g, c):
                    at, m = CH[c]
                    n = g * NC + c
                    if c == 0:
                        pe.wait_ge(xn_ready, g + 1)
                    if n >= 2:
                        pe.wait_ge(hid_ready, n - 1)
                    nc.tensor.matmul(g_ps[0:m, n % 2, :], w1[:, HID + at:HID + at + m], xnT[:, g % 2, :],
                                     start=True, stop=True)
                    nc.tensor.matmul(a_ps[0:m, n % 2, :], w1[:, at:at + m], xnT[:, g % 2, :],
                                     start=True, stop=True).then_inc(up_done, 1)

                def down(g):
                    pe.wait_ge(hid_ready, (g + 1) * NC)
                    if g >= 2:
                        pe.wait_ge(h_added, g - 1)
                    for q in range(NT):
                        to = y_ps[:, g % 2, q * P:(q + 1) * P]
                        for c, (at, m) in enumerate(CH):
                            ins = nc.tensor.matmul(to, hid[0:m, g % 2, c, q * P:(q + 1) * P], w2[0:m, c, :],
                                                   start=(c == 0), stop=(c == NC - 1))
                    ins.then_inc(down_done, 1)

                up(0)
                for g in range(G):
                    for c in range(NC):
                        if c == 1 and g + 1 < G:
                            up(g + 1)
                        hidden(g, c)
                    if g >= 1:
                        down(g - 1)
                down(G - 1)

            @block.scalar
            def _(act):
                def affine(g):
                    act.wait_ge(x_turned, g + 1)
                    if g >= 2:
                        act.wait_ge(up_done, (g - 1) * NC)
                    nc.scalar.activation(xnT[:, g % 2, :], x_ps[:], ACT.Identity, bias=gb[:, 1:2],
                                         scale=gb[:, 0:1]).then_inc(xn_ready, 1)

                affine(0)
                for g in range(G):
                    for c, (at, m) in enumerate(CH):
                        n = g * NC + c
                        act.wait_ge(up_done, n + 1)
                        if n >= 2:
                            act.wait_ge(hid_ready, n - 1)
                        nc.scalar.activation(gate[0:m, n % 2, :], g_ps[0:m, n % 2, :], ACT.Gelu,
                                             bias=b1[0:m, NC + c:NC + c + 1]).then_inc(gate_ready, 1)
                        if c == 1 and g + 1 < G:
                            affine(g + 1)

            @block.vector
            def _(dve):
                def normalise(g):
                    if g >= 2:
                        dve.wait_ge(x_turned, g - 1)
                    for j in range(NT):
                        t = (b + g) * NT + j
                        ins = nc.vector.tensor_scalar(xs[:, g % 2, j, :], XH[:, bass.ds(t, 1), :],
                                                      mean[:, bass.ds(t, 1)], rstd[:, bass.ds(t, 1)],
                                                      ALU.subtract, ALU.mult)
                    ins.then_inc(xs_ready, 1)

                def add(g):
                    dve.wait_ge(down_done, g + 1)
                    dve.wait_ge(b2_added, g + 1)
                    mine = H[:, bass.ds((b + g) * NT, NT), :]
                    nc.vector.tensor_tensor(mine, y_ps[:, g % 2, :].rearrange("p (j d) -> p j d", j=NT), mine,
                                            ALU.add).then_inc(h_added, 1)

                normalise(0)
                normalise(1)
                for g in range(G):
                    for c, (at, m) in enumerate(CH):
                        n = g * NC + c
                        dve.wait_ge(gate_ready, n + 1)
                        if g >= 2 and c == 0:
                            dve.wait_ge(down_done, g - 1)
                        nc.vector.scalar_tensor_tensor(hid[0:m, g % 2, c, :], a_ps[0:m, n % 2, :], b1[0:m, c:c + 1],
                                                       gate[0:m, n % 2, :], ALU.add, ALU.mult).then_inc(hid_ready, 1)
                        if c == 0 and g >= 2:
                            add(g - 2)
                    if g + 2 < G:
                        normalise(g + 2)
                add(G - 2)
                add(G - 1)

        clear_counts(nc, sems)


def build(nc, x, gamma, beta, Wq, Wk, Wv, Wo, wqkv, q_scale, k_scale, wo, ln_g, ln_b, w1, b1, w2, b2,
          c_ident, c_dist, c_mask, c_rope, out):
    NC = len(CH)
    ctx = ExitStack()
    with ctx:
        def sb(name, shape, c=ctx):
            return c.enter_context(nc.sbuf_tensor(name, shape, F32))

        X = sb("X", [P, TILES, D])
        ident = sb("ident", [P, P])
        mean = sb("mean", [P, TILES])
        rstd = sb("rstd", [P, TILES])
        loaded = ctx.enter_context(nc.semaphore("loaded"))
        x_dram = x.rearrange("b (j p) d -> p (b j) d", p=P)
        out_dram = out.rearrange("b (j p) d -> p (b j) d", p=P)

        with ExitStack() as c1:
            dist = sb("dist", [P, DW], c1)
            gb = sb("gb", [P, 2], c1)
            wqkv1 = sb("wqkv1", [P, 3 * NH * DH], c1)
            wo1 = sb("wo1", [P, NPAIR, D], c1)
            Q = TILES // 4
            x_loaded = [c1.enter_context(nc.semaphore(f"x_loaded_{i}")) for i in range(4)]

            def load(sp):
                for i in range(4):
                    sp.dma_start(X[:, i * Q:(i + 1) * Q, :], x_dram[:, i * Q:(i + 1) * Q, :]).then_inc(x_loaded[i], 16)
                loads = [(ident[:], c_ident), (dist[:], c_dist),
                         (gb[:, 0:1], gamma.rearrange("(p o) -> p o", o=1)),
                         (gb[:, 1:2], beta.rearrange("(p o) -> p o", o=1)),
                         (wqkv1[:, 0:1024], Wq), (wqkv1[:, 1024:2048], Wk), (wqkv1[:, 2048:3072], Wv),
                         (wo1[:], Wo.rearrange("(c p) d -> p c d", p=P))]
                for to, of in loads:
                    sp.dma_start(to, of).then_inc(loaded, 16)
                sp.wait_ge(loaded, 16 * len(loads))

            def arrive(dve, t):
                if t % Q == 0:
                    dve.wait_ge(x_loaded[t // Q], 16)

            layer_stats(nc, c1, "ln1", X, mean, rstd, True, load, arrive)
            global_attention(nc, c1, X, mean, rstd, ident, dist, gb, wqkv1, wo1)

        with ExitStack() as c2:
            H = sb("H", [P, TILES, D], c2)
            normed = c2.enter_context(nc.semaphore("normed"))

            def local_buffers(layer):
                tag = f"l{layer}_"
                c3 = ExitStack()
                mask = sb(tag + "mask", [P, 2, P], c3)
                rope = sb(tag + "rope", [P, NT, 4, DH], c3)
                scl = sb(tag + "scl", [P, 4, DH], c3)
                wl = sb(tag + "wl", [P, 3 * S], c3)
                wol = sb(tag + "wol", [P, FPAIR, D], c3)
                ld = c3.enter_context(nc.semaphore(tag + "ld"))

                def load(sp):
                    loads = [(mask[:], c_mask), (rope[:], c_rope), (wl[:], wqkv[layer]),
                             (wol[:], wo[layer].rearrange("(c p) d -> p c d", p=P))]
                    HF = DH // 2
                    for n, v in enumerate((q_scale, k_scale)):
                        row = v[layer:layer + 1, :]
                        loads += [(scl[:, n, :], row.broadcast_to([P, DH])),
                                  (scl[:, 2 + n, 0:HF], row[:, HF:DH].broadcast_to([P, HF])),
                                  (scl[:, 2 + n, HF:DH], row[:, 0:HF].broadcast_to([P, HF]))]
                    for to, of in loads:
                        sp.dma_start(to, of).then_inc(ld, 16)
                    sp.wait_ge(ld, 16 * len(loads))

                return c3, mask, rope, scl, wl, wol, load

            local = local_buffers(0)
            layer_stats(nc, c2, "ln2", X, mean, rstd, False, local[-1])
            with nc.Block() as block:
                @block.vector
                def _(dve):
                    for t in range(TILES):
                        ins = nc.vector.tensor_scalar(H[:, t, :], X[:, t, :], mean[:, t:t + 1], rstd[:, t:t + 1],
                                                      ALU.subtract, ALU.mult)
                    ins.then_inc(normed, 1)
                    dve.wait_ge(normed, 1)
            for layer in range(DEPTH):
                tag = f"l{layer}_"
                c3, mask, rope, scl, wl, wol, _ = local
                with c3:
                    local_attention(nc, c3, tag, H, ident, mask, rope, scl, wl, wol)
                if layer + 1 < DEPTH:
                    local = local_buffers(layer + 1)
                with ExitStack() as c4:
                    XH = sb(tag + "XH", [P, TILES, D], c4)
                    gbl = sb(tag + "gbl", [P, 2], c4)
                    w1l = sb(tag + "w1l", [P, 2 * HID], c4)
                    b1l = sb(tag + "b1l", [P, 2 * NC], c4)
                    w2l = sb(tag + "w2l", [P, NC, D], c4)
                    b2l = sb(tag + "b2l", [P, 1, D], c4)
                    ld = c4.enter_context(nc.semaphore(tag + "ld2"))
                    filled = c4.enter_context(nc.semaphore(tag + "filled"))
                    Q = TILES // 4
                    shifted = [c4.enter_context(nc.semaphore(f"{tag}shifted_{i}")) for i in range(4)]
                    HF = D // 2

                    def load(sp):
                        for i in range(4):
                            mine = slice(i * Q, (i + 1) * Q)
                            sp.dma_start(XH[1:P, mine, HF:D], H[0:P - 1, mine, HF:D]).then_inc(shifted[i], 16)
                            early = XH[0:1, mine, HF:D].rearrange("p (b j) d -> p b j d", j=NT)
                            late = H[P - 1:P, mine, HF:D].rearrange("p (b j) d -> p b j d", j=NT)
                            for j in range(1, NT):
                                sp.dma_start(early[:, :, j, :], late[:, :, j - 1, :]).then_inc(shifted[i], 16)
                        g = "(p o) -> p o"
                        loads = [(gbl[:, 0:1], ln_g[layer].rearrange(g, o=1)),
                                 (gbl[:, 1:2], ln_b[layer].rearrange(g, o=1)),
                                 (w1l[:], w1[layer]), (b2l[:, 0, :], b2[layer:layer + 1, :].broadcast_to([P, D]))]
                        for c, (at, m) in enumerate(CH):
                            loads += [(b1l[0:m, c:c + 1], b1[layer, at:at + m].rearrange(g, o=1)),
                                      (b1l[0:m, NC + c:NC + c + 1],
                                       b1[layer, HID + at:HID + at + m].rearrange(g, o=1)),
                                      (w2l[0:m, c, :], w2[layer, at:at + m, :])]
                        for to, of in loads:
                            sp.dma_start(to, of).then_inc(ld, 16)
                        sp.wait_ge(ld, 16 * len(loads))
                        if layer + 1 < DEPTH:
                            local[-1](sp)

                    def arrive(dve, t):
                        if t == 0:
                            nc.vector.memset(XH[0:1, 0:TILES:NT, HF:D], 0.0)
                            nc.vector.tensor_copy(XH[:, :, 0:HF], H[:, :, 0:HF]).then_inc(filled, 1)
                            dve.wait_ge(filled, 1)
                        if t % Q == 0:
                            dve.wait_ge(shifted[t // Q], 16 * NT)

                    layer_stats(nc, c4, tag + "ln", XH, mean, rstd, False, load, arrive)
                    gated_mlp(nc, c4, tag, H, XH, mean, rstd, ident, gbl, w1l, b1l, w2l, b2l)
            summed = c2.enter_context(nc.semaphore("summed"))
            stored = c2.enter_context(nc.semaphore("stored"))
            Q = TILES // 4
            with nc.Block() as block:
                @block.vector
                def _(dve):
                    for i in range(4):
                        s = slice(i * Q, (i + 1) * Q)
                        nc.vector.tensor_tensor(X[:, s, :], X[:, s, :], H[:, s, :], ALU.add).then_inc(summed, 1)

                @block.sync
                def _(sp):
                    for i in range(4):
                        s = slice(i * Q, (i + 1) * Q)
                        sp.wait_ge(summed, i + 1)
                        sp.dma_start(out_dram[:, s, :], X[:, s, :]).then_inc(stored, 16)
                    sp.wait_ge(stored, 64)


def constants():
    import numpy as np
    p = np.arange(P)
    ident = np.eye(P, dtype=np.float32)
    dist = np.abs(p[:, None] + (NT - 1) * P - np.arange(DW)[None, :]).astype(np.float32)
    i, j = (p % W)[:, None], np.arange(2 * W)[None, :]
    ok = (j <= i + W) & (j >= i)
    first = ok & ~((p[:, None] < W) & (j < W))
    swapped = np.where(p[:, None] < W, (np.arange(P)[None, :] + W) % P, np.arange(P)[None, :])
    ok, first = np.take_along_axis(ok, swapped, 1), np.take_along_axis(first, swapped, 1)
    mask = np.stack([np.where(first, 0, -1e30), np.where(ok, 0, -1e30)], 1).astype(np.float32)
    half = np.arange(0, DH, 2, dtype=np.float32)
    inv = (1.0 / 10000.0 ** (half / DH)).astype(np.float32)
    t = np.arange(S, dtype=np.float32)
    f = (t[:, None] * inv[None, :]).astype(np.float32)
    f = np.concatenate([f, f], -1)
    base = ((half + np.float32(0.4 * DH)) / np.float32(1.4 * DH)).astype(np.float32)
    power = (t - S // 2) / np.float32(W // 2)
    sc = (base[None, :] ** power[:, None]).astype(np.float32)
    sc = np.concatenate([sc, sc], -1)
    cos, sin = np.cos(f), np.sin(f)
    sin = np.concatenate([-sin[:, :DH // 2], sin[:, DH // 2:]], -1)
    rope = np.stack([8.0 * cos * sc, cos / sc, 8.0 * sin * sc, sin / sc], 1).astype(np.float32)
    rope = rope.reshape(NT, P, 4, DH).transpose(1, 0, 2, 3).copy()
    return {"c_ident": ident, "c_dist": dist, "c_mask": mask, "c_rope": rope}


_INS = ["L0_attn_x", "L0_attn_ln_gamma", "L0_attn_ln_beta", "L0_attn_Wq", "L0_attn_Wk", "L0_attn_Wv", "L0_attn_Wo",
        "L0_ffn_wqkv", "L0_ffn_q_scale", "L0_ffn_k_scale", "L0_ffn_wo", "L0_ffn_ln_g", "L0_ffn_ln_b", "L0_ffn_w1",
        "L0_ffn_b1", "L0_ffn_w2", "L0_ffn_b2"]


def kernel(**inputs):
    import numpy as _np
    import concourse.bacc as _bacc
    from concourse import mybir as _mybir
    from concourse.bass_utils import run_bass_kernel_spmd as _run

    nc = _bacc.Bacc("TRN2", target_bir_lowering=False, num_devices=1)
    arrays, args = {}, []
    given = [(n, _np.ascontiguousarray(inputs[n])) for n in _INS] + list(constants().items())
    for name, a in given:
        arrays[f"in_{name}_dram"] = a
        args.append(nc.dram_tensor(f"in_{name}_dram", a.shape, _mybir.dt.from_np(a.dtype), kind="ExternalInput").ap())
    args.append(nc.dram_tensor("out_0_dram", (NB, S, D), _mybir.dt.float32, kind="ExternalOutput").ap())
    build(nc, *args)
    r = _run(nc, [arrays], core_ids=[0])
    return r.results[0]["out_0_dram"]
```
